# Optimizing a Trainium2 kernel written in Bass

```python
import numpy as np
import jax
import jax.numpy as jnp

def _softmax(x, axis=-1):
    return jax.nn.softmax(x, axis=axis)

def _gelu(x):
    return jax.nn.gelu(x, approximate=True)

def _silu(x):
    return jax.nn.silu(x)

def _sigmoid(x):
    return jax.nn.sigmoid(x)

def _layernorm(x, axis=-1, eps=1e-05):
    m = jnp.mean(x, axis=axis, keepdims=True)
    v = jnp.var(x, axis=axis, keepdims=True)
    return (x - m) / jnp.sqrt(v + eps)

def _scatter_add(tgt, idx, src, axis=0):
    return tgt.at[idx].add(src)

def _segment_sum(src, seg, n):
    return jax.ops.segment_sum(src, seg, n)
kernel_name = 'mk_dlrm_tower_d1_rec_r8_ccbee2'

def setup_inputs(seed: int=0):
    np.random.seed(seed)
    _w = jnp.asarray

    def _rec_inputs():
        import jax
        import jax.numpy as jnp
        _tk = jax.random.key(seed)
        dense_ctx = jax.random.normal(jax.random.fold_in(_tk, 190), (2048, 16), jnp.float32)
        ids = jnp.stack([jax.random.randint(jax.random.fold_in(_tk, 200 + f), (2048,), 0, v, jnp.int32) for f, v in enumerate([1000, 1000, 1000, 1000, 12500, 125000, 1000, 12500, 1250, 125000, 1000, 125000, 1250, 1250, 1000, 1000, 12500, 12500, 1000, 125000, 12500, 12500, 1000, 125000, 1000, 1250, 1000, 1000, 1000, 12500, 1250, 1250])], axis=1)
        tbl_0 = 0.05 * jax.random.normal(jax.random.fold_in(_tk, 500 + 0), (1000, 16), jnp.float32)
        tbl_1 = 0.05 * jax.random.normal(jax.random.fold_in(_tk, 500 + 1), (1000, 16), jnp.float32)
        tbl_2 = 0.05 * jax.random.normal(jax.random.fold_in(_tk, 500 + 2), (1000, 16), jnp.float32)
        tbl_3 = 0.05 * jax.random.normal(jax.random.fold_in(_tk, 500 + 3), (1000, 16), jnp.float32)
        tbl_4 = 0.05 * jax.random.normal(jax.random.fold_in(_tk, 500 + 4), (12500, 16), jnp.float32)
        tbl_5 = 0.05 * jax.random.normal(jax.random.fold_in(_tk, 500 + 5), (125000, 16), jnp.float32)
        tbl_6 = 0.05 * jax.random.normal(jax.random.fold_in(_tk, 500 + 6), (1000, 16), jnp.float32)
        tbl_7 = 0.05 * jax.random.normal(jax.random.fold_in(_tk, 500 + 7), (12500, 16), jnp.float32)
        tbl_8 = 0.05 * jax.random.normal(jax.random.fold_in(_tk, 500 + 8), (1250, 16), jnp.float32)
        tbl_9 = 0.05 * jax.random.normal(jax.random.fold_in(_tk, 500 + 9), (125000, 16), jnp.float32)
        tbl_10 = 0.05 * jax.random.normal(jax.random.fold_in(_tk, 500 + 10), (1000, 16), jnp.float32)
        tbl_11 = 0.05 * jax.random.normal(jax.random.fold_in(_tk, 500 + 11), (125000, 16), jnp.float32)
        tbl_12 = 0.05 * jax.random.normal(jax.random.fold_in(_tk, 500 + 12), (1250, 16), jnp.float32)
        tbl_13 = 0.05 * jax.random.normal(jax.random.fold_in(_tk, 500 + 13), (1250, 16), jnp.float32)
        tbl_14 = 0.05 * jax.random.normal(jax.random.fold_in(_tk, 500 + 14), (1000, 16), jnp.float32)
        tbl_15 = 0.05 * jax.random.normal(jax.random.fold_in(_tk, 500 + 15), (1000, 16), jnp.float32)
        tbl_16 = 0.05 * jax.random.normal(jax.random.fold_in(_tk, 500 + 16), (12500, 16), jnp.float32)
        tbl_17 = 0.05 * jax.random.normal(jax.random.fold_in(_tk, 500 + 17), (12500, 16), jnp.float32)
        tbl_18 = 0.05 * jax.random.normal(jax.random.fold_in(_tk, 500 + 18), (1000, 16), jnp.float32)
        tbl_19 = 0.05 * jax.random.normal(jax.random.fold_in(_tk, 500 + 19), (125000, 16), jnp.float32)
        tbl_20 = 0.05 * jax.random.normal(jax.random.fold_in(_tk, 500 + 20), (12500, 16), jnp.float32)
        tbl_21 = 0.05 * jax.random.normal(jax.random.fold_in(_tk, 500 + 21), (12500, 16), jnp.float32)
        tbl_22 = 0.05 * jax.random.normal(jax.random.fold_in(_tk, 500 + 22), (1000, 16), jnp.float32)
        tbl_23 = 0.05 * jax.random.normal(jax.random.fold_in(_tk, 500 + 23), (125000, 16), jnp.float32)
        tbl_24 = 0.05 * jax.random.normal(jax.random.fold_in(_tk, 500 + 24), (1000, 16), jnp.float32)
        tbl_25 = 0.05 * jax.random.normal(jax.random.fold_in(_tk, 500 + 25), (1250, 16), jnp.float32)
        tbl_26 = 0.05 * jax.random.normal(jax.random.fold_in(_tk, 500 + 26), (1000, 16), jnp.float32)
        tbl_27 = 0.05 * jax.random.normal(jax.random.fold_in(_tk, 500 + 27), (1000, 16), jnp.float32)
        tbl_28 = 0.05 * jax.random.normal(jax.random.fold_in(_tk, 500 + 28), (1000, 16), jnp.float32)
        tbl_29 = 0.05 * jax.random.normal(jax.random.fold_in(_tk, 500 + 29), (12500, 16), jnp.float32)
        tbl_30 = 0.05 * jax.random.normal(jax.random.fold_in(_tk, 500 + 30), (1250, 16), jnp.float32)
        tbl_31 = 0.05 * jax.random.normal(jax.random.fold_in(_tk, 500 + 31), (1250, 16), jnp.float32)
        _rk = jax.random.fold_in(_tk, 7)
        W_top1 = 0.0606339 * jax.random.normal(jax.random.fold_in(_tk, 801), (272, 512), jnp.float32)
        W_top2 = 0.0441942 * jax.random.normal(jax.random.fold_in(_tk, 802), (512, 256), jnp.float32)
        W_top3 = 0.0625 * jax.random.normal(jax.random.fold_in(_tk, 803), (256, 1), jnp.float32)
        b_top1 = jnp.zeros((512,), jnp.float32)
        b_top2 = jnp.zeros((256,), jnp.float32)
        return (dense_ctx, ids, tbl_0, tbl_1, tbl_2, tbl_3, tbl_4, tbl_5, tbl_6, tbl_7, tbl_8, tbl_9, tbl_10, tbl_11, tbl_12, tbl_13, tbl_14, tbl_15, tbl_16, tbl_17, tbl_18, tbl_19, tbl_20, tbl_21, tbl_22, tbl_23, tbl_24, tbl_25, tbl_26, tbl_27, tbl_28, tbl_29, tbl_30, tbl_31, W_top1, b_top1, W_top2, b_top2, W_top3)
    dense_ctx, ids, tbl_0, tbl_1, tbl_2, tbl_3, tbl_4, tbl_5, tbl_6, tbl_7, tbl_8, tbl_9, tbl_10, tbl_11, tbl_12, tbl_13, tbl_14, tbl_15, tbl_16, tbl_17, tbl_18, tbl_19, tbl_20, tbl_21, tbl_22, tbl_23, tbl_24, tbl_25, tbl_26, tbl_27, tbl_28, tbl_29, tbl_30, tbl_31, W_top1, b_top1, W_top2, b_top2, W_top3 = _rec_inputs()

    def _L0_rec_setup():
        import jax, jax.numpy as jnp
        import numpy as np
        NUM_FIELDS = 32
        EMBED_DIM = 16
        BATCH = 512
        CROSS_SIZES = [128, 128, 128]

        def _cin_forward(x, Ws, bs):
            x0 = x
            h = x
            xs = []
            n_layers = len(Ws)
            for i in range(n_layers):
                B, F, E = x0.shape
                G = h.shape[1]
                z = (x0[:, :, None, :] * h[:, None, :, :]).reshape(B, F * G, E)
                y = jax.nn.relu(jnp.einsum('oc,bce->boe', Ws[i], z) + bs[i][None, :, None])
                if i != n_layers - 1:
                    half = y.shape[1] // 2
                    x_keep, h = (y[:, :half, :], y[:, half:, :])
                else:
                    x_keep, h = (y, y)
                xs.append(x_keep)
            return jnp.sum(jnp.concatenate(xs, axis=1), axis=2)
        key = jax.random.key(seed)
        ks = jax.random.split(key, 8)
        x = jax.random.normal(ks[0], (BATCH, NUM_FIELDS, EMBED_DIM), dtype=jnp.float32)
        prev = NUM_FIELDS
        inp = {'x': x}
        for i, cs in enumerate(CROSS_SIZES):
            in_ch = NUM_FIELDS * prev
            scale = 1.0 / np.sqrt(in_ch)
            inp[f'W{i}'] = jax.random.uniform(ks[1 + 2 * i], (cs, in_ch), dtype=jnp.float32, minval=-scale, maxval=scale)
            inp[f'b{i}'] = jax.random.uniform(ks[2 + 2 * i], (cs,), dtype=jnp.float32, minval=-scale, maxval=scale)
            prev = cs // 2
        return inp
    _L0_rec_all = _L0_rec_setup()
    _L0_rec_in = {k: v for k, v in _L0_rec_all.items() if k in ('W0', 'b0', 'W1', 'b1', 'W2', 'b2')}
    del _L0_rec_all
    return {'dense_ctx': dense_ctx, 'ids': ids, 'tbl_0': tbl_0, 'tbl_1': tbl_1, 'tbl_2': tbl_2, 'tbl_3': tbl_3, 'tbl_4': tbl_4, 'tbl_5': tbl_5, 'tbl_6': tbl_6, 'tbl_7': tbl_7, 'tbl_8': tbl_8, 'tbl_9': tbl_9, 'tbl_10': tbl_10, 'tbl_11': tbl_11, 'tbl_12': tbl_12, 'tbl_13': tbl_13, 'tbl_14': tbl_14, 'tbl_15': tbl_15, 'tbl_16': tbl_16, 'tbl_17': tbl_17, 'tbl_18': tbl_18, 'tbl_19': tbl_19, 'tbl_20': tbl_20, 'tbl_21': tbl_21, 'tbl_22': tbl_22, 'tbl_23': tbl_23, 'tbl_24': tbl_24, 'tbl_25': tbl_25, 'tbl_26': tbl_26, 'tbl_27': tbl_27, 'tbl_28': tbl_28, 'tbl_29': tbl_29, 'tbl_30': tbl_30, 'tbl_31': tbl_31, 'W_top1': W_top1, 'b_top1': b_top1, 'W_top2': W_top2, 'b_top2': b_top2, 'W_top3': W_top3, 'L0_rec_W0': _L0_rec_in['W0'], 'L0_rec_b0': _L0_rec_in['b0'], 'L0_rec_W1': _L0_rec_in['W1'], 'L0_rec_b1': _L0_rec_in['b1'], 'L0_rec_W2': _L0_rec_in['W2'], 'L0_rec_b2': _L0_rec_in['b2']}

def reference(dense_ctx, ids, tbl_0, tbl_1, tbl_2, tbl_3, tbl_4, tbl_5, tbl_6, tbl_7, tbl_8, tbl_9, tbl_10, tbl_11, tbl_12, tbl_13, tbl_14, tbl_15, tbl_16, tbl_17, tbl_18, tbl_19, tbl_20, tbl_21, tbl_22, tbl_23, tbl_24, tbl_25, tbl_26, tbl_27, tbl_28, tbl_29, tbl_30, tbl_31, W_top1, b_top1, W_top2, b_top2, W_top3, L0_rec_W0, L0_rec_b0, L0_rec_W1, L0_rec_b1, L0_rec_W2, L0_rec_b2):
    import jax
    import jax.numpy as jnp

    def _L0_rec_ref(x, W0, b0, W1, b1, W2, b2):
        import jax, jax.numpy as jnp
        import numpy as np
        NUM_FIELDS = 32
        EMBED_DIM = 16
        BATCH = 512
        CROSS_SIZES = [128, 128, 128]

        def _cin_forward(x, Ws, bs):
            x0 = x
            h = x
            xs = []
            n_layers = len(Ws)
            for i in range(n_layers):
                B, F, E = x0.shape
                G = h.shape[1]
                z = (x0[:, :, None, :] * h[:, None, :, :]).reshape(B, F * G, E)
                y = jax.nn.relu(jnp.einsum('oc,bce->boe', Ws[i], z) + bs[i][None, :, None])
                if i != n_layers - 1:
                    half = y.shape[1] // 2
                    x_keep, h = (y[:, :half, :], y[:, half:, :])
                else:
                    x_keep, h = (y, y)
                xs.append(x_keep)
            return jnp.sum(jnp.concatenate(xs, axis=1), axis=2)
        return _cin_forward(x, [W0, W1, W2], [b0, b1, b2])
    e = jnp.stack([tbl_0[ids[:, 0]], tbl_1[ids[:, 1]], tbl_2[ids[:, 2]], tbl_3[ids[:, 3]], tbl_4[ids[:, 4]], tbl_5[ids[:, 5]], tbl_6[ids[:, 6]], tbl_7[ids[:, 7]], tbl_8[ids[:, 8]], tbl_9[ids[:, 9]], tbl_10[ids[:, 10]], tbl_11[ids[:, 11]], tbl_12[ids[:, 12]], tbl_13[ids[:, 13]], tbl_14[ids[:, 14]], tbl_15[ids[:, 15]], tbl_16[ids[:, 16]], tbl_17[ids[:, 17]], tbl_18[ids[:, 18]], tbl_19[ids[:, 19]], tbl_20[ids[:, 20]], tbl_21[ids[:, 21]], tbl_22[ids[:, 22]], tbl_23[ids[:, 23]], tbl_24[ids[:, 24]], tbl_25[ids[:, 25]], tbl_26[ids[:, 26]], tbl_27[ids[:, 27]], tbl_28[ids[:, 28]], tbl_29[ids[:, 29]], tbl_30[ids[:, 30]], tbl_31[ids[:, 31]]], axis=1)
    z = _L0_rec_ref(e, L0_rec_W0, L0_rec_b0, L0_rec_W1, L0_rec_b1, L0_rec_W2, L0_rec_b2)
    z = z.reshape(z.shape[0], -1)
    h = jnp.concatenate([z, dense_ctx], axis=1)
    h = jnp.maximum(h @ W_top1 + b_top1, 0.0)
    h = jnp.maximum(h @ W_top2 + b_top2, 0.0)
    y = h @ W_top3
    return y

_drawn_inputs = setup_inputs


def setup_inputs(seed=0):
    import zlib

    import numpy as np

    out = dict(_drawn_inputs(seed))
    spreads = {'b_top1': (0.0, 0.353), 'b_top2': (0.0, 0.402)}
    factors = {'tbl_0': 8.0,
     'tbl_1': 8.0,
     'tbl_2': 8.0,
     'tbl_3': 8.0,
     'tbl_4': 8.0,
     'tbl_5': 8.0,
     'tbl_6': 8.0,
     'tbl_7': 8.0,
     'tbl_8': 8.0,
     'tbl_9': 8.0,
     'tbl_10': 8.0,
     'tbl_11': 8.0,
     'tbl_12': 8.0,
     'tbl_13': 8.0,
     'tbl_14': 8.0,
     'tbl_15': 8.0,
     'tbl_16': 8.0,
     'tbl_17': 8.0,
     'tbl_18': 8.0,
     'tbl_19': 8.0,
     'tbl_20': 8.0,
     'tbl_21': 8.0,
     'tbl_22': 8.0,
     'tbl_23': 8.0,
     'tbl_24': 8.0,
     'tbl_25': 8.0,
     'tbl_26': 8.0,
     'tbl_27': 8.0,
     'tbl_28': 8.0,
     'tbl_29': 8.0,
     'tbl_30': 8.0,
     'tbl_31': 8.0,
     'L0_rec_W0': 8.0,
     'L0_rec_W1': 8.0,
     'L0_rec_W2': 8.0,
     'L0_rec_b0': 4.863,
     'L0_rec_b1': 7.136,
     'L0_rec_b2': 7.496}
    for name, (base, spread) in spreads.items():
        noise = np.random.default_rng([zlib.crc32(name.encode()), seed]).standard_normal(out[name].shape)
        drawn = base * np.exp(spread * noise) if base else spread * noise
        out[name] = jnp.asarray(drawn.astype(out[name].dtype))
    for name, factor in factors.items():
        out[name] = (out[name] * factor).astype(out[name].dtype)
    return out
```

```python
from contextlib import ExitStack

import numpy as np

import concourse.bass as bass
import concourse.mybir as mybir
from concourse.alu_op_type import AluOpType as ALU

ACT = mybir.ActivationFunctionType
AX = mybir.AxisListType
F32 = mybir.dt.float32
BF16 = mybir.dt.bfloat16
I32 = mybir.dt.int32

P = 128
BATCH = 2048
FIELDS = 32
EMBED = 16
CROSS = 128
HALF = CROSS // 2
DENSE = 16
TOP1, TOP2 = 512, 256

TILES = BATCH // P
BLOCKS = 4
ROWS = P // BLOCKS
TOK = ROWS * EMBED

KT = FIELDS * HALF // P
GROUPS = 4
PAIRS = KT // 2
KT0 = 5
ZRING = 4

PARTS = 4
FL = FIELDS // GROUPS
MLP_CHUNKS = BATCH // 512


def build(nc, ids, tables, dense_t, w0a, w0b, w1, w2, bias, wt1, wt2, wt3, bt1, bt2, sel, out):
    with ExitStack() as ctx:
        def sb(name, shape, dt=F32):
            return ctx.enter_context(nc.sbuf_tensor(name, shape, dt))

        def sem(name):
            return ctx.enter_context(nc.semaphore(name))

        w0_sb = sb("w0_sb", [P, KT0, CROSS])
        w0b_sb = sb("w0b_sb", [P, KT0, CROSS])
        w1_sb = sb("w1_sb", [P, KT, CROSS])
        w2_sb = sb("w2_sb", [P, KT, CROSS])
        bias_sb = sb("bias_sb", [P, 5])
        wt1_sb = sb("wt1_sb", [P, 3, TOP1])
        wt2_sb = sb("wt2_sb", [P, TOP1 // P, TOP2])
        wt3_sb = sb("wt3_sb", [P, TOP2 // P])
        bt1_sb = sb("bt1_sb", [P, TOP1 // P])
        bt2_sb = sb("bt2_sb", [P, TOP2 // P])
        dense_sb = sb("dense_sb", [DENSE, BATCH])
        sel_sb = sb("sel_sb", [P, 10, P], BF16)
        sel_rep = sel_sb[:, 0:4, :]
        sel_x4 = sel_sb[:, 4, :]
        sel_shift = sel_sb[:, 5:9, :]
        ident = sel_sb[:, 9, :]

        ids_sb = sb("ids_sb", [P, FIELDS], I32)
        emb = sb("emb", [P, FIELDS * EMBED])
        rest = sb("rest", [P, EMBED, GROUPS, FL])
        parts = sb("parts", [P, EMBED, GROUPS, PARTS, FL], BF16)
        xs = sb("xs", [P, P, EMBED], BF16)

        x4 = sb("x4", [P, TOK])
        xrep = sb("xrep", [P, 2, GROUPS, GROUPS, TOK])
        z0 = sb("z0", [P, 4, TOK])
        zsq = sb("zsq", [P, TOK])
        z = sb("z", [P, ZRING, 2, TOK])
        h0 = sb("h0", [P, TOK])
        h1 = sb("h1", [P, TOK])
        y01 = sb("y01", [P, 2, TOK])
        y2 = sb("y2", [P, 2, TOK])

        cin01 = sb("cin01", [P, BATCH])
        cin2 = sb("cin2", [P, BATCH])
        xrep_flat = xrep[:, :, :, :, :].rearrange("p a b c t -> p (a b c t)")
        m1 = xrep_flat[:, 0:4 * BATCH].rearrange("p (m b) -> p m b", m=4)
        m2 = xrep_flat[:, 4 * BATCH:6 * BATCH].rearrange("p (m b) -> p m b", m=2)
        sel_f32 = xrep_flat[:, 0:10 * P].rearrange("p (m c) -> p m c", m=10)
        y_sb = xrep_flat[0:1, 6 * BATCH:7 * BATCH]

        psum = ctx.enter_context(nc.psum_tensor("psum", [P, 8, 512], F32))
        spread = psum[:, 0:4, :]
        acc0, acc1, acc2 = psum[:, 4, :], psum[:, 5, :], psum[:, 6, :]
        misc = psum[:, 7, :]
        turned = misc.bitcast(BF16).rearrange("p (e b) -> p e b", e=8)

        s_sel, s_w0, s_bias = sem("s_sel"), sem("s_w0"), sem("s_bias")
        s_w1, s_w2, s_top = sem("s_w1"), sem("s_w2"), sem("s_top")
        ids_loaded = sem("ids_loaded")
        tiles_begun = sem("tiles_begun")
        gathered = sem("gathered")
        parts_zeroed = sem("parts_zeroed")
        cut = sem("cut")
        turned_done = sem("turned_done")
        xs_ready = sem("xs_ready")
        sel_cast = sem("sel_cast")
        w0_summed = sem("w0_summed")
        x4_spread = sem("x4_spread")
        x4_ready = sem("x4_ready")
        zsq_ready = sem("zsq_ready")
        shift_spread = sem("shift_spread")
        z0_ready = sem("z0_ready")
        rep_spread = sem("rep_spread")
        rep_ready = sem("rep_ready")
        z_ready = sem("z_ready")
        z_used = sem("z_used")
        l0_done, l1_done, l2_done = sem("l0_done"), sem("l1_done"), sem("l2_done")
        h0_ready, h1_ready = sem("h0_ready"), sem("h1_ready")
        y0_ready = sem("y0_ready")
        y1_ready = sem("y1_ready")
        y2_ready = sem("y2_ready")
        y01_summed, y2_summed = sem("y01_summed"), sem("y2_summed")
        m1_acc, m1_ready = sem("m1_acc"), sem("m1_ready")
        m2_acc, m2_ready = sem("m2_acc"), sem("m2_ready")
        m3_acc, m3_ready = sem("m3_acc"), sem("m3_ready")
        stored = sem("stored")

        def wait(eng, semaphore, value):
            if not isinstance(value, int) or value > 0:
                eng.wait_ge(semaphore, value)

        def all_steps(eng, step):
            for i in range(BLOCKS):
                step(0, i, False)
            with eng.Fori(1, TILES - 1) as t:
                for i in range(BLOCKS):
                    step(t, i, False)
            for i in range(BLOCKS):
                step(TILES - 1, i, i == BLOCKS - 1)

        block = ctx.enter_context(nc.Block())

        @block.sync
        def _(sp):
            ids_v = ids.rearrange("(t p) f -> t p f", p=P)
            sp.dma_start(ids_sb[:, :], ids_v[0]).then_inc(ids_loaded, 16)
            sp.dma_start(sel_f32, sel).then_inc(s_sel, 16)
            sp.dma_start(w0_sb[:, :, :], w0a).then_inc(s_w0, 16)
            sp.dma_start(w0b_sb[:, :, :], w0b).then_inc(s_w0, 16)
            sp.dma_start(bias_sb[:, :], bias).then_inc(s_bias, 16)
            sp.dma_start(w1_sb[:, :, :], w1).then_inc(s_w1, 16)
            sp.dma_start(w2_sb[:, :, :], w2).then_inc(s_w2, 16)
            for k in range(2):
                sp.dma_start(wt1_sb[:, k, :], wt1[k * P:(k + 1) * P, :]).then_inc(s_top, 16)
            sp.dma_start(wt1_sb[0:DENSE, 2, :], wt1[2 * P:2 * P + DENSE, :]).then_inc(s_top, 16)
            sp.dma_start(wt2_sb[:, :, :], wt2.rearrange("(k p) n -> p k n", p=P)).then_inc(s_top, 16)
            sp.dma_start(wt3_sb[:, :], wt3).then_inc(s_top, 16)
            sp.dma_start(bt1_sb[:, :], bt1).then_inc(s_top, 16)
            sp.dma_start(bt2_sb[:, :], bt2).then_inc(s_top, 16)
            sp.dma_start(dense_sb[:, :], dense_t).then_inc(s_top, 16)
            with sp.Fori(1, TILES) as t:
                sp.wait_ge(gathered, t * (16 * FIELDS))
                sp.wait_ge(cut, 4 * t - 2)
                sp.dma_start(ids_sb[:, :], ids[bass.ts(t, P), :]).then_inc(ids_loaded, 16)
            for c in range(MLP_CHUNKS):
                sp.wait_ge(m3_ready, c + 1)
                sp.dma_start(out[0:1, bass.ts(c, 512)], y_sb[:, bass.ts(c, 512)]).then_inc(stored, 16)
            sp.wait_ge(stored, 16 * MLP_CHUNKS)

        @block.gpsimd
        def _(pool):
            pool.memset(parts[:, :, :, 3, :], 0.0).then_inc(parts_zeroed, 1)

            def gather_fields():
                for f in range(FIELDS):
                    pool.indirect_dma_start(
                        out=emb[:, f * EMBED:(f + 1) * EMBED], out_offset=None,
                        in_=tables[f], in_offset=bass.IndirectOffsetOnAxis(ids_sb[:, f:f + 1], 0),
                    ).then_inc(gathered, 16)

            pool.wait_ge(ids_loaded, 16)
            gather_fields()
            with pool.Fori(1, TILES) as t:
                pool.wait_ge(ids_loaded, 16 * t + 16)
                pool.sem_inc(tiles_begun, 1)
                gather_fields()

        @block.tensor
        def _(pe):
            def turn(t, half):
                pe.wait_ge(cut, 4 * t + 4)
                if half == 0:
                    wait(pe, zsq_ready, BLOCKS * t)
                else:
                    pe.wait_ge(xs_ready, 2 * t + 1)
                for e in range(8):
                    lane = parts[:, 8 * half + e].rearrange("p a b c -> p (a b c)")
                    mm = pe.transpose(turned[:, e, :], lane, ident)
                mm.then_inc(turned_done, 1)

            def tokens(n, i, lo, hi):
                return xs[lo:hi, ROWS * i:ROWS * (i + 1), :].rearrange("p b e -> p (b e)")

            def spread_x4(t, i):
                n = BLOCKS * t + i
                pe.wait_ge(xs_ready, 2 * t + 2)
                wait(pe, zsq_ready, n)
                pe.matmul(misc, sel_x4, tokens(n, i, 0, P), start=True, stop=True).then_inc(x4_spread, 1)

            def spread_shift(t, i):
                n = BLOCKS * t + i
                wait(pe, rep_ready, GROUPS * n)
                for j in range(4):
                    mm = pe.matmul(spread[:, j, :], sel_shift[:, j, :], tokens(n, i, 0, P),
                                   start=True, stop=True)
                mm.then_inc(shift_spread, 1)

            def spread_rep(t, i, g):
                n = BLOCKS * t + i
                if g == 0:
                    pe.wait_ge(z0_ready, 2 * n + 2)
                else:
                    pe.wait_ge(rep_ready, GROUPS * n + g)
                for r in range(GROUPS):
                    lo, hi = 32 * r, 32 * (r + 1)
                    mm = pe.matmul(spread[:, r, :], sel_rep[lo:hi, g, :], tokens(n, i, lo, hi),
                                   start=True, stop=True)
                mm.then_inc(rep_spread, 1)

            def layer0(n):
                pe.wait_ge(zsq_ready, n + 1)
                wait(pe, y0_ready, n)
                pe.matmul(acc0, w0_sb[:, 4, :], zsq[:, :], start=True, stop=False)
                for j in range(4):
                    if j % 2 == 0:
                        pe.wait_ge(z0_ready, 2 * n + j // 2 + 1)
                    mm = pe.matmul(acc0, w0_sb[:, j, :], z0[:, j, :], start=False, stop=(j == 3))
                mm.then_inc(l0_done, 1)

            def pair(n, layer, p):
                acc, w = (acc1, w1_sb) if layer == 1 else (acc2, w2_sb)
                q = 2 * PAIRS * n + PAIRS * (layer - 1) + p
                if p == 0:
                    wait(pe, y1_ready if layer == 1 else y2_ready, n)
                pe.wait_ge(z_ready, q + 1)
                for m in range(2):
                    k = 4 * (2 * (p % 2) + m) + p // 2
                    mm = pe.matmul(acc, w[:, k, :], z[:, (PAIRS * (layer - 1) + p) % ZRING, m, :],
                                   start=(p == 0 and m == 0), stop=(p == PAIRS - 1 and m == 1))
                return mm.then_inc(z_used, 1)

            def step(t, i, last):
                n = BLOCKS * t + i
                nt, ni = (t, i + 1) if i + 1 < BLOCKS else (t + 1, 0)
                for p in range(PAIRS):
                    if ni == 0 and not last and p in (0, 2):
                        turn(nt, p // 2)
                    if not last and p == 4:
                        spread_x4(nt, ni)
                    if not last and p == 5:
                        spread_shift(nt, ni)
                    pair(n, 1, p)
                if not last:
                    layer0(n + 1)
                for p in range(PAIRS):
                    if not last and p % 2 == 0:
                        spread_rep(nt, ni, p // 2)
                    pair(n, 2, p)

            pe.wait_ge(sel_cast, 1)
            turn(0, 0)
            turn(0, 1)
            spread_x4(0, 0)
            spread_shift(0, 0)
            pe.wait_ge(w0_summed, 1)
            layer0(0)
            for g in range(GROUPS):
                spread_rep(0, 0, g)
            pe.wait_ge(s_w1, 16)
            pe.wait_ge(s_w2, 16)
            all_steps(pe, step)

            pe.wait_ge(s_top, 16 * 8)
            pe.wait_ge(y01_summed, BLOCKS * TILES)
            pe.wait_ge(y2_summed, BLOCKS * TILES)
            for c in range(MLP_CHUNKS):
                rows = bass.ts(c, 512)
                for m in range(TOP1 // P):
                    g = 4 * c + m
                    wait(pe, m1_ready, g - 7)
                    cols = bass.ts(m, P)
                    pe.matmul(psum[:, g % 8, :], wt1_sb[:, 0, cols], cin01[:, rows], start=True, stop=False)
                    pe.matmul(psum[:, g % 8, :], wt1_sb[:, 1, cols], cin2[:, rows], start=False, stop=False)
                    pe.matmul(psum[:, g % 8, :], wt1_sb[0:DENSE, 2, cols], dense_sb[:, rows],
                              start=False, stop=True).then_inc(m1_acc, 1)
            for c in range(MLP_CHUNKS):
                rows = bass.ts(c, 512)
                pe.wait_ge(m1_ready, 4 * (c + 1))
                for m in range(TOP2 // P):
                    g = 2 * c + m
                    pe.wait_ge(m1_ready, 8 + g + 1)
                    for k in range(4):
                        mm = pe.matmul(psum[:, g, :], wt2_sb[:, k, bass.ts(m, P)], m1[:, k, rows],
                                       start=(k == 0), stop=(k == 3))
                    mm.then_inc(m2_acc, 1)
            for c in range(MLP_CHUNKS):
                pe.wait_ge(m2_ready, 2 * (c + 1))
                for k in range(2):
                    mm = pe.matmul(psum[0:1, c, :], wt3_sb[:, k:k + 1], m2[:, k, bass.ts(c, 512)],
                                   start=(k == 0), stop=(k == 1))
                mm.then_inc(m3_acc, 1)

        @block.scalar
        def _(act):
            def xs_half(t, half):
                act.wait_ge(turned_done, 2 * t + half + 1)
                act.activation(xs[:, :, 8 * half:8 * half + 8].rearrange("p b e -> p e b"), turned,
                               ACT.Copy).then_inc(xs_ready, 1)

            def take_x4(n):
                act.wait_ge(x4_spread, n + 1)
                wait(act, z0_ready, 2 * n)
                act.activation(x4[:, :], misc, ACT.Copy).then_inc(x4_ready, 1)
                wait(act, l0_done, n)
                act.activation(zsq[:, :], misc, ACT.Square).then_inc(zsq_ready, 1)

            def take_rep(n, par, g):
                act.wait_ge(rep_spread, GROUPS * n + g + 1)
                if g == 0:
                    wait(act, z_ready, 2 * PAIRS * (n - 1))
                act.activation(xrep[:, par, g, :, :], spread, ACT.Copy).then_inc(rep_ready, 1)

            def relu(out_, in_, b):
                return act.activation(out_, in_, ACT.Relu, bias=b)

            def end_layer0(n, par):
                act.wait_ge(l0_done, n + 1)
                wait(act, z_ready, 2 * PAIRS * n - PAIRS)
                relu(h0[HALF:P, :], acc0[HALF:P, :], bias_sb[HALF:P, 1:2])
                relu(h0[0:HALF, :], acc0[HALF:P, :], bias_sb[HALF:P, 1:2]).then_inc(h0_ready, 1)
                wait(act, y01_summed, n - 1)
                relu(y01[0:HALF, par, :], acc0[0:HALF, :], bias_sb[0:HALF, 0:1]).then_inc(y0_ready, 1)

            def end_layer1(n, par):
                act.wait_ge(z_used, 2 * PAIRS * n + PAIRS)
                wait(act, z_ready, 2 * PAIRS * n)
                relu(h1[0:HALF, :], acc1[0:HALF, :], bias_sb[0:HALF, 3:4])
                relu(h1[HALF:P, :], acc1[0:HALF, :], bias_sb[0:HALF, 3:4]).then_inc(h1_ready, 1)
                relu(y01[HALF:P, par, :], acc1[HALF:P, :], bias_sb[HALF:P, 2:3]).then_inc(y1_ready, 1)

            def end_layer2(n, par):
                act.wait_ge(z_used, 2 * PAIRS * (n + 1))
                wait(act, y2_summed, n - 1)
                relu(y2[:, par, :], acc2, bias_sb[:, 4:5]).then_inc(y2_ready, 1)

            def step(t, i, last):
                n = BLOCKS * t + i
                if not last:
                    if i == BLOCKS - 1:
                        xs_half(t + 1, 0)
                        xs_half(t + 1, 1)
                    take_x4(n + 1)
                end_layer1(n, i % 2)
                if not last:
                    take_rep(n + 1, (i + 1) % 2, 0)
                    end_layer0(n + 1, (i + 1) % 2)
                    for g in range(1, GROUPS):
                        take_rep(n + 1, (i + 1) % 2, g)
                end_layer2(n, i % 2)

            act.wait_ge(s_bias, 16)
            xs_half(0, 0)
            xs_half(0, 1)
            take_x4(0)
            end_layer0(0, 0)
            act.wait_ge(sel_cast, 1)
            for g in range(GROUPS):
                take_rep(0, 0, g)
            all_steps(act, step)

            act.wait_ge(s_top, 16 * 8)
            for g in range(4 * MLP_CHUNKS):
                c, m = divmod(g, 4)
                act.wait_ge(m1_acc, g + 1)
                relu(m1[:, m, bass.ts(c, 512)], psum[:, g % 8, :], bt1_sb[:, m:m + 1]).then_inc(m1_ready, 1)
            for g in range(2 * MLP_CHUNKS):
                c, m = divmod(g, 2)
                act.wait_ge(m2_acc, g + 1)
                relu(m2[:, m, bass.ts(c, 512)], psum[:, g, :], bt2_sb[:, m:m + 1]).then_inc(m2_ready, 1)
            for c in range(MLP_CHUNKS):
                act.wait_ge(m3_acc, c + 1)
                act.activation(y_sb[:, bass.ts(c, 512)], psum[0:1, c, :], ACT.Copy).then_inc(m3_ready, 1)

        @block.vector
        def _(dve):
            emb_v = emb[:, :].rearrange("p (r c e) -> p e r c", r=GROUPS, c=FL)

            def cut_parts(t):
                dve.wait_ge(gathered, 16 * FIELDS * (t + 1))
                wait(dve, turned_done, 2 * t)
                dve.tensor_copy(parts[:, :, :, 0, :], emb_v).then_inc(cut, 1)
                dve.wait_ge(cut, 4 * t + 1)
                dve.tensor_tensor(rest[:, :, :, :], emb_v, parts[:, :, :, 0, :], ALU.subtract).then_inc(cut, 1)
                dve.wait_ge(cut, 4 * t + 2)
                dve.tensor_copy(parts[:, :, :, 1, :], rest[:, :, :, :]).then_inc(cut, 1)
                dve.wait_ge(cut, 4 * t + 3)
                dve.tensor_tensor(parts[:, :, :, 2, :], rest[:, :, :, :], parts[:, :, :, 1, :],
                                  ALU.subtract).then_inc(cut, 1)

            def shift_products(n):
                dve.wait_ge(shift_spread, n + 1)
                dve.wait_ge(x4_ready, n + 1)
                wait(dve, l0_done, n)
                for j in range(2):
                    dve.tensor_tensor(z0[:, 2 * j:2 * j + 2, :], spread[:, 2 * j:2 * j + 2, :],
                                      x4[:, :].unsqueeze(1).broadcast_to([P, 2, TOK]),
                                      ALU.mult).then_inc(z0_ready, 1)

            def product(n, par, layer, p):
                q = 2 * PAIRS * n + PAIRS * (layer - 1) + p
                h, ready = (h0, h0_ready) if layer == 1 else (h1, h1_ready)
                if p == 0:
                    dve.wait_ge(ready, n + 1)
                if layer == 1 and p % 2 == 0:
                    dve.wait_ge(rep_ready, GROUPS * n + p // 2 + 1)
                wait(dve, z_used, q - ZRING + 1)
                m = 2 * (p % 2)
                dve.tensor_tensor(z[:, (PAIRS * (layer - 1) + p) % ZRING, :, :],
                                  xrep[:, par, p // 2, m:m + 2, :],
                                  h[:, :].unsqueeze(1).broadcast_to([P, 2, TOK]),
                                  ALU.mult).then_inc(z_ready, 1)

            def lane_sum(dst, n, src, done):
                dve.tensor_reduce(dst[:, bass.ts(n, ROWS)], src.rearrange("p (b e) -> p b e", e=EMBED),
                                  AX.X, ALU.add).then_inc(done, 1)

            def step(t, i, last):
                n = BLOCKS * t + i
                for p in range(PAIRS):
                    product(n, i % 2, 1, p)
                    if p == 5 and not (isinstance(n, int) and n == 0):
                        dve.wait_ge(y2_ready, n)
                        lane_sum(cin2, n - 1, y2[:, (i + 1) % 2, :], y2_summed)
                if not last:
                    shift_products(n + 1)
                for p in range(PAIRS):
                    product(n, i % 2, 2, p)
                    if p == 1:
                        dve.wait_ge(y0_ready, n + 1)
                        dve.wait_ge(y1_ready, n + 1)
                        lane_sum(cin01, n, y01[:, i % 2, :], y01_summed)
                    if p == 3 and i == 2 and not (isinstance(t, int) and t == TILES - 1):
                        cut_parts(t + 1)

            dve.wait_ge(s_sel, 16)
            dve.tensor_copy(sel_sb[:, :, :], sel_f32).then_inc(sel_cast, 1)
            dve.wait_ge(s_w0, 32)
            dve.wait_ge(parts_zeroed, 1)
            dve.tensor_tensor(w0_sb[:, :, :], w0_sb[:, :, :], w0b_sb[:, :, :], ALU.add).then_inc(w0_summed, 1)
            cut_parts(0)
            shift_products(0)
            all_steps(dve, step)
            dve.wait_ge(y2_ready, BLOCKS * TILES)
            lane_sum(cin2, BLOCKS * TILES - 1, y2[:, 1, :], y2_summed)


def _selections():
    part = np.arange(P) % 32 // FL
    field = FL * (np.arange(P) // 32) + np.arange(P) % FL
    col = np.arange(P)
    live = (part < 3)[:, None]
    mats = [live & ((np.arange(P) % FL)[:, None] == 2 * g + col[None, :] // HALF) for g in range(4)]
    mats.append(live & (field[:, None] == col[None, :] % FIELDS))
    mats += [live & (field[:, None] == (col[None, :] % FIELDS + 4 * j + col[None, :] // FIELDS + 1) % FIELDS)
             for j in range(4)]
    mats.append(col[:, None] == col[None, :])
    return np.ascontiguousarray(np.stack(mats, axis=1).astype(np.float32))


def _shifted_weights(w0):
    w = w0.reshape(CROSS, FIELDS, FIELDS)
    f = np.arange(FIELDS)
    a = np.zeros((KT0, P, CROSS), w0.dtype)
    b = np.zeros((KT0, P, CROSS), w0.dtype)
    for s in range(1, 17):
        j, row = (s - 1) // 4, FIELDS * ((s - 1) % 4)
        a[j, row:row + FIELDS] = w[:, f, (f + s) % FIELDS].T
        if s < 16:
            b[j, row:row + FIELDS] = w[:, (f + s) % FIELDS, f].T
    a[4, 0:FIELDS] = w[:, f, f].T
    return [np.ascontiguousarray(x.transpose(1, 0, 2)) for x in (a, b)]


def kernel(**inputs):
    import concourse.bacc as bacc
    from concourse.bass_utils import run_bass_kernel_spmd

    x = {k: np.asarray(v) for k, v in inputs.items()}
    turn = np.r_[HALF:CROSS, 0:HALF]

    def by_ktile(w):
        return np.ascontiguousarray(w.T.reshape(KT, P, CROSS).transpose(1, 0, 2))

    w0a, w0b = _shifted_weights(x["L0_rec_W0"])
    b0, b1, b2 = x["L0_rec_b0"], x["L0_rec_b1"], x["L0_rec_b2"]
    bias = np.stack([np.r_[b0[:HALF], b0[:HALF]], np.r_[b0[HALF:], b0[HALF:]],
                     np.r_[b1[:HALF], b1[:HALF]], np.r_[b1[HALF:], b1[HALF:]], b2], axis=1)
    arrays = {
        "ids": x["ids"],
        "dense_t": np.ascontiguousarray(x["dense_ctx"].T),
        "w0a": w0a, "w0b": w0b,
        "w1": by_ktile(x["L0_rec_W1"][turn]),
        "w2": by_ktile(x["L0_rec_W2"]),
        "bias": np.ascontiguousarray(bias),
        "wt1": x["W_top1"], "wt2": x["W_top2"],
        "wt3": np.ascontiguousarray(x["W_top3"].reshape(TOP2 // P, P).T),
        "bt1": np.ascontiguousarray(x["b_top1"].reshape(TOP1 // P, P).T),
        "bt2": np.ascontiguousarray(x["b_top2"].reshape(TOP2 // P, P).T),
        "sel": _selections(),
    }
    for f in range(FIELDS):
        arrays[f"tbl_{f}"] = x[f"tbl_{f}"]

    nc = bacc.Bacc("TRN2", target_bir_lowering=False, num_devices=1)
    aps = {k: nc.dram_tensor(k, a.shape, mybir.dt.from_np(a.dtype), kind="ExternalInput").ap()
           for k, a in arrays.items()}
    tables = [aps.pop(f"tbl_{f}") for f in range(FIELDS)]
    out = nc.dram_tensor("out", (1, BATCH), F32, kind="ExternalOutput").ap()
    build(nc, tables=tables, out=out, **aps)
    r = run_bass_kernel_spmd(nc, [arrays], core_ids=[0])
    return np.asarray(r.results[0]["out"]).reshape(BATCH, 1)
```

```python
from contextlib import ExitStack

import numpy as np

import concourse.bass as bass
import concourse.mybir as mybir
from concourse.alu_op_type import AluOpType as ALU

ACT = mybir.ActivationFunctionType
AX = mybir.AxisListType
F32 = mybir.dt.float32
F32R = mybir.dt.float32r
BF16 = mybir.dt.bfloat16
I32 = mybir.dt.int32

P = 128
BATCH = 2048
FIELDS = 32
EMBED = 16
CROSS = 128
HALF = CROSS // 2
DENSE = 16
TOP1, TOP2 = 512, 256

TILES = BATCH // P
BLOCKS = 4
ROWS = P // BLOCKS
TOK = ROWS * EMBED

KT = FIELDS * HALF // P
GROUPS = 4
PAIRS = KT // 2
KT0 = 5
STEPS = TILES * BLOCKS + 1

ITEMS = ([(1, 0), (1, 1), (1, 2)] + [x for p in range(5) for x in ((2, p), (1, p + 3))]
         + [(2, 5), (2, 6), (2, 7)])
L1_END, L2_END = ITEMS.index((1, PAIRS - 1)), ITEMS.index((2, PAIRS - 1))
RING = 4

PE_TURN, PE_X4, PE_SHIFT, PE_LAYER0 = 1, 3, 4, 9
PE_REP = {9: 0, 11: 1, 13: 2, 15: 3}
DVE_Z0 = {7: 0, 8: 1}
DVE_SUM01, DVE_SUM2, DVE_CUT = 4, 10, 11

PARTS = 4
FL = FIELDS // GROUPS
MLP_CHUNKS = BATCH // 512


def build(nc, ids, tables, dense_t, w0a, w0b, w_even, w_odd_d, bias, wt1, wt2, wt3, bt1, bt2, sel, out):
    with ExitStack() as ctx:
        def sb(name, shape, dt=F32):
            return ctx.enter_context(nc.sbuf_tensor(name, shape, dt))

        def sem(name):
            return ctx.enter_context(nc.semaphore(name))

        w0_sb = sb("w0_sb", [P, KT0, CROSS])
        w_full = sb("w_full", [P, 8, 2, CROSS])
        w_hi = sb("w_hi", [P, 8, 2, CROSS], F32R)
        w_lo = sb("w_lo", [P, 8, 2, CROSS], F32R)
        bias_sb = sb("bias_sb", [P, 5])
        wt3_sb = sb("wt3_sb", [P, TOP2 // P])
        bt1_sb = sb("bt1_sb", [P, TOP1 // P])
        bt2_sb = sb("bt2_sb", [P, TOP2 // P])
        sel_sb = sb("sel_sb", [P, 10, P], BF16)
        sel_rep = sel_sb[:, 0:4, :]
        sel_x4 = sel_sb[:, 4, :]
        sel_shift = sel_sb[:, 5:9, :]
        ident = sel_sb[:, 9, :]

        ids_sb = sb("ids_sb", [P, FIELDS], I32)
        emb = sb("emb", [P, FIELDS * EMBED])
        rest = sb("rest", [P, EMBED, GROUPS, FL])
        parts = sb("parts", [P, EMBED, GROUPS, PARTS, FL], BF16)
        xs = sb("xs", [P, P, EMBED], BF16)

        x4 = sb("x4", [P, TOK])
        xrep = sb("xrep", [P, 2, GROUPS, GROUPS, TOK])
        z0 = sb("z0", [P, 4, TOK])
        zsq = sb("zsq", [P, TOK])
        z_full = sb("z_full", [P, RING, 2, TOK])
        z_cut = sb("z_cut", [P, 2, 2, TOK])
        z_hi = sb("z_hi", [P, RING, 2, TOK], F32R)
        z_lo = sb("z_lo", [P, RING, 2, TOK], F32R)
        h0 = sb("h0", [P, 2, TOK])
        h1 = sb("h1", [P, TOK])
        y01 = sb("y01", [P, 2, TOK])
        y2 = sb("y2", [P, TOK])

        cin01 = sb("cin01", [P, BATCH])
        cin2 = sb("cin2", [P, BATCH])

        even = xrep[:, 0, :, :, :].rearrange("p b c t -> p (b c t)")
        odd = xrep[:, 1, :, :, :].rearrange("p b c t -> p (b c t)")
        sel_f32 = odd[:, 0:10 * P].rearrange("p (m c) -> p m c", m=10)
        w0b_sb = odd[:, 10 * P:(10 + KT0) * P].rearrange("p (k c) -> p k c", k=KT0)
        w_odd = odd[:, 2048:4096].rearrange("p (i m c) -> p i m c", i=8, m=2)
        wt1_sb = even[:, 0:3 * TOP1].rearrange("p (k n) -> p k n", k=3)
        wt2_sb = even[:, 2048:2048 + 4 * TOP2].rearrange("p (k n) -> p k n", k=4)
        dense_sb = even[0:DENSE, 4096:4096 + BATCH]
        y_sb = even[0:1, 6144:6144 + BATCH]
        m1 = odd.rearrange("p (m b) -> p m b", m=4)
        m2 = z_full[:, :, :, :].rearrange("p a m t -> p (a m t)").rearrange("p (m b) -> p m b", m=2)

        psum = ctx.enter_context(nc.psum_tensor("psum", [P, 8, 512], F32))
        spread = psum[:, 0:4, :]
        acc0, acc1, acc2 = psum[:, 4, :], psum[:, 5, :], psum[:, 6, :]
        misc = psum[:, 7, :]
        turned = [x.bitcast(BF16).rearrange("p (e b) -> p e b", e=8) for x in (misc, psum[:, 0, :])]

        s_sel, s_w0, s_bias = sem("s_sel"), sem("s_w0"), sem("s_bias")
        s_w, s_top = sem("s_w"), sem("s_top")
        ids_loaded = sem("ids_loaded")
        tiles_begun = sem("tiles_begun")
        gathered = sem("gathered")
        parts_zeroed = sem("parts_zeroed")
        cut = sem("cut")
        turned_done = sem("turned_done")
        xs_ready = sem("xs_ready")
        sel_cast = sem("sel_cast")
        w0_summed = sem("w0_summed")
        w_hi_ready = sem("w_hi_ready")
        w_lo_ready = sem("w_lo_ready")
        x4_spread = sem("x4_spread")
        x4_ready = sem("x4_ready")
        zsq_ready = sem("zsq_ready")
        shift_spread = sem("shift_spread")
        z0_ready = sem("z0_ready")
        rep_spread = sem("rep_spread")
        rep_ready = sem("rep_ready")
        z_ready = sem("z_ready")
        hi_ready = sem("hi_ready")
        lo_ready = sem("lo_ready")
        z_used = sem("z_used")
        l0_done = sem("l0_done")
        h0_ready, h1_ready = sem("h0_ready"), sem("h1_ready")
        y0_ready = sem("y0_ready")
        y1_ready = sem("y1_ready")
        y2_ready = sem("y2_ready")
        y01_summed, y2_summed = sem("y01_summed"), sem("y2_summed")
        m1_acc, m1_ready = sem("m1_acc"), sem("m1_ready")
        m2_acc, m2_ready = sem("m2_acc"), sem("m2_ready")
        m3_acc, m3_ready = sem("m3_acc"), sem("m3_ready")
        stored = sem("stored")

        def wait(eng, semaphore, value):
            if not isinstance(value, int) or value > 0:
                eng.wait_ge(semaphore, value)

        def live(b, it):
            return not (isinstance(b, int) and (b == 0 and ITEMS[it][0] == 2
                                                or b == STEPS - 1 and ITEMS[it][0] == 1))

        def items_until(b, it, odd_only=False):
            if it < 0:
                b, it = b - 1, it + len(ITEMS)
            if isinstance(b, int) and b < 0:
                return 0
            first, per = sum(live(0, j) for j in picked(odd_only)), len(picked(odd_only))
            here = sum(live(b, j) for j in picked(odd_only) if j <= it)
            return here if isinstance(b, int) and b == 0 else per * (b - 1) + first + here

        def picked(odd_only):
            return range(1, len(ITEMS), 2) if odd_only else range(len(ITEMS))

        block = ctx.enter_context(nc.Block())

        @block.sync
        def _(sp):
            ids_v = ids.rearrange("(t p) f -> t p f", p=P)
            sp.dma_start(ids_sb[:, :], ids_v[0]).then_inc(ids_loaded, 16)
            sp.dma_start(sel_f32, sel).then_inc(s_sel, 16)
            sp.dma_start(w0_sb[:, :, :], w0a).then_inc(s_w0, 16)
            sp.dma_start(w0b_sb, w0b).then_inc(s_w0, 16)
            sp.dma_start(bias_sb[:, :], bias).then_inc(s_bias, 16)
            sp.dma_start(w_full[:, :, :, :], w_even).then_inc(s_w, 16)
            sp.dma_start(w_odd, w_odd_d).then_inc(s_w, 16)
            sp.dma_start(wt3_sb[:, :], wt3).then_inc(s_top, 16)
            sp.dma_start(bt1_sb[:, :], bt1).then_inc(s_top, 16)
            sp.dma_start(bt2_sb[:, :], bt2).then_inc(s_top, 16)
            with sp.Fori(1, TILES) as t:
                sp.wait_ge(gathered, t * (16 * FIELDS))
                sp.wait_ge(cut, 4 * t - 2)
                sp.dma_start(ids_sb[:, :], ids[bass.ts(t, P), :]).then_inc(ids_loaded, 16)
            sp.wait_ge(z_ready, items_until(STEPS - 2, L2_END))
            for k in range(2):
                sp.dma_start(wt1_sb[:, k, :], wt1[k * P:(k + 1) * P, :]).then_inc(s_top, 16)
            sp.dma_start(wt1_sb[0:DENSE, 2, :], wt1[2 * P:2 * P + DENSE, :]).then_inc(s_top, 16)
            sp.dma_start(wt2_sb, wt2.rearrange("(k p) n -> p k n", p=P)).then_inc(s_top, 16)
            sp.dma_start(dense_sb, dense_t).then_inc(s_top, 16)
            for c in range(MLP_CHUNKS):
                sp.wait_ge(m3_ready, c + 1)
                sp.dma_start(out[0:1, bass.ts(c, 512)], y_sb[:, bass.ts(c, 512)]).then_inc(stored, 16)
            sp.wait_ge(stored, 16 * MLP_CHUNKS)

        @block.gpsimd
        def _(pool):
            pool.memset(parts[:, :, :, 3, :], 0.0).then_inc(parts_zeroed, 1)

            def gather_fields():
                for f in range(FIELDS):
                    pool.indirect_dma_start(
                        out=emb[:, f * EMBED:(f + 1) * EMBED], out_offset=None,
                        in_=tables[f], in_offset=bass.IndirectOffsetOnAxis(ids_sb[:, f:f + 1], 0),
                    ).then_inc(gathered, 16)

            pool.wait_ge(ids_loaded, 16)
            gather_fields()
            with pool.Fori(1, TILES) as t:
                pool.wait_ge(ids_loaded, 16 * t + 16)
                pool.sem_inc(tiles_begun, 1)
                gather_fields()

        @block.tensor
        def _(pe):
            def turn(t):
                pe.wait_ge(cut, 4 * t + 4)
                wait(pe, zsq_ready, BLOCKS * t)
                wait(pe, rep_ready, GROUPS * BLOCKS * t)
                for e in range(EMBED):
                    lane = parts[:, e].rearrange("p a b c -> p (a b c)")
                    mm = pe.transpose(turned[e // 8][:, e % 8, :], lane, ident)
                mm.then_inc(turned_done, 1)

            def tokens(i, lo, hi):
                return xs[lo:hi, ROWS * i:ROWS * (i + 1), :].rearrange("p b e -> p (b e)")

            def spread_x4(t, i, n):
                pe.wait_ge(xs_ready, 2 * t + 2)
                wait(pe, zsq_ready, n)
                pe.matmul(misc, sel_x4, tokens(i, 0, P), start=True, stop=True).then_inc(x4_spread, 1)

            def spread_shift(i, n):
                wait(pe, rep_ready, GROUPS * n)
                for j in range(4):
                    mm = pe.matmul(spread[:, j, :], sel_shift[:, j, :], tokens(i, 0, P),
                                   start=True, stop=True)
                mm.then_inc(shift_spread, 1)

            def spread_rep(i, n, g):
                if g == 0:
                    pe.wait_ge(z0_ready, 2 * n + 2)
                else:
                    pe.wait_ge(rep_ready, GROUPS * n + g)
                for r in range(GROUPS):
                    lo, hi = 32 * r, 32 * (r + 1)
                    mm = pe.matmul(spread[:, r, :], sel_rep[lo:hi, g, :], tokens(i, lo, hi),
                                   start=True, stop=True)
                mm.then_inc(rep_spread, 1)

            def layer0(n):
                pe.wait_ge(zsq_ready, n + 1)
                wait(pe, y0_ready, n)
                pe.matmul(acc0, w0_sb[:, 4, :], zsq[:, :], start=True, stop=False)
                for j in range(4):
                    if j % 2 == 0:
                        pe.wait_ge(z0_ready, 2 * n + j // 2 + 1)
                    mm = pe.matmul(acc0, w0_sb[:, j, :], z0[:, j, :], start=False, stop=(j == 3))
                mm.then_inc(l0_done, 1)

            def contract(b, it):
                layer, p = ITEMS[it]
                acc = acc1 if layer == 1 else acc2
                if p == 0 and layer == 1:
                    wait(pe, y1_ready, b)
                if p == 0 and layer == 2:
                    wait(pe, y2_ready, b - 1)
                first, last, slot = p == 0, p == PAIRS - 1, it // 2
                if it % 2 == 0:
                    pe.wait_ge(z_ready, items_until(b, it))
                    for m in range(2):
                        mm = pe.matmul(acc, w_full[:, slot, m, :], z_full[:, slot % RING, m, :],
                                       start=(first and m == 0), stop=(last and m == 1))
                else:
                    pe.wait_ge(hi_ready, items_until(b, it, odd_only=True))
                    for m in range(2):
                        pe.matmul(acc, w_hi[:, slot, m, :], z_hi[:, slot % RING, m, :],
                                  start=(first and m == 0), stop=False)
                        pe.matmul(acc, w_lo[:, slot, m, :], z_hi[:, slot % RING, m, :],
                                  start=False, stop=False)
                    pe.wait_ge(lo_ready, items_until(b, it, odd_only=True))
                    for m in range(2):
                        mm = pe.matmul(acc, w_hi[:, slot, m, :], z_lo[:, slot % RING, m, :],
                                       start=False, stop=(last and m == 1))
                mm.then_inc(z_used, 1)

            def step(t, i, b):
                nt, ni = (t, i + 1) if i + 1 < BLOCKS else (t + 1, 0)
                more = not (isinstance(b, int) and b + 1 >= BLOCKS * TILES)
                for it in range(len(ITEMS)):
                    if more and it == PE_TURN and ni == 0:
                        turn(nt)
                    if more and it == PE_X4:
                        spread_x4(nt, ni, b + 1)
                    if more and it == PE_SHIFT:
                        spread_shift(ni, b + 1)
                    if more and it == PE_LAYER0:
                        layer0(b + 1)
                    if more and it in PE_REP:
                        spread_rep(ni, b + 1, PE_REP[it])
                    if live(b, it):
                        contract(b, it)

            pe.wait_ge(sel_cast, 1)
            turn(0)
            spread_x4(0, 0, 0)
            spread_shift(0, 0)
            pe.wait_ge(w0_summed, 1)
            layer0(0)
            for g in range(GROUPS):
                spread_rep(0, 0, g)
            pe.wait_ge(s_w, 32)
            pe.wait_ge(w_lo_ready, 1)
            for i in range(BLOCKS):
                step(0, i, i)
            with pe.Fori(1, TILES - 1) as t:
                for i in range(BLOCKS):
                    step(t, i, BLOCKS * t + i)
            for b in range(STEPS - 1 - BLOCKS, STEPS):
                step(b // BLOCKS, b % BLOCKS, b)

            pe.wait_ge(s_top, 16 * 8)
            pe.wait_ge(y01_summed, BLOCKS * TILES)
            pe.wait_ge(y2_summed, BLOCKS * TILES)
            for c in range(MLP_CHUNKS):
                rows = bass.ts(c, 512)
                for m in range(TOP1 // P):
                    g = 4 * c + m
                    wait(pe, m1_ready, g - 7)
                    cols = bass.ts(m, P)
                    pe.matmul(psum[:, g % 8, :], wt1_sb[:, 0, cols], cin01[:, rows], start=True, stop=False)
                    pe.matmul(psum[:, g % 8, :], wt1_sb[:, 1, cols], cin2[:, rows], start=False, stop=False)
                    pe.matmul(psum[:, g % 8, :], wt1_sb[0:DENSE, 2, cols], dense_sb[:, rows],
                              start=False, stop=True).then_inc(m1_acc, 1)
            for c in range(MLP_CHUNKS):
                rows = bass.ts(c, 512)
                pe.wait_ge(m1_ready, 4 * (c + 1))
                for m in range(TOP2 // P):
                    g = 2 * c + m
                    pe.wait_ge(m1_ready, 8 + g + 1)
                    for k in range(4):
                        mm = pe.matmul(psum[:, g, :], wt2_sb[:, k, bass.ts(m, P)], m1[:, k, rows],
                                       start=(k == 0), stop=(k == 3))
                    mm.then_inc(m2_acc, 1)
            for c in range(MLP_CHUNKS):
                pe.wait_ge(m2_ready, 2 * (c + 1))
                for k in range(2):
                    mm = pe.matmul(psum[0:1, c, :], wt3_sb[:, k:k + 1], m2[:, k, bass.ts(c, 512)],
                                   start=(k == 0), stop=(k == 1))
                mm.then_inc(m3_acc, 1)

        @block.scalar
        def _(act):
            def take_xs(t):
                act.wait_ge(turned_done, t + 1)
                for half in range(2):
                    act.activation(xs[:, :, 8 * half:8 * half + 8].rearrange("p b e -> p e b"),
                                   turned[half], ACT.Copy).then_inc(xs_ready, 1)

            def take_x4(n):
                act.wait_ge(x4_spread, n + 1)
                wait(act, z0_ready, 2 * n)
                act.activation(x4[:, :], misc, ACT.Copy).then_inc(x4_ready, 1)
                wait(act, l0_done, n)
                act.activation(zsq[:, :], misc, ACT.Square).then_inc(zsq_ready, 1)

            def take_rep(n, par, g):
                act.wait_ge(rep_spread, GROUPS * n + g + 1)
                wait(act, z_ready, items_until(n - 1, ITEMS.index((2, 2 * g + 1))))
                act.activation(xrep[:, par, g, :, :], spread, ACT.Copy).then_inc(rep_ready, 1)

            def relu(out_, in_, b):
                return act.activation(out_, in_, ACT.Relu, bias=b)

            def end_layer0(n, par):
                act.wait_ge(l0_done, n + 1)
                wait(act, z_ready, items_until(n - 2, L1_END))
                relu(h0[HALF:P, par, :], acc0[HALF:P, :], bias_sb[HALF:P, 1:2])
                relu(h0[0:HALF, par, :], acc0[HALF:P, :], bias_sb[HALF:P, 1:2]).then_inc(h0_ready, 1)
                wait(act, y01_summed, n - 1)
                relu(y01[0:HALF, par, :], acc0[0:HALF, :], bias_sb[0:HALF, 0:1]).then_inc(y0_ready, 1)

            def end_layer1(n, par):
                act.wait_ge(z_used, items_until(n, L1_END))
                wait(act, z_ready, items_until(n, L2_END))
                relu(h1[0:HALF, :], acc1[0:HALF, :], bias_sb[0:HALF, 3:4])
                relu(h1[HALF:P, :], acc1[0:HALF, :], bias_sb[0:HALF, 3:4]).then_inc(h1_ready, 1)
                relu(y01[HALF:P, par, :], acc1[HALF:P, :], bias_sb[HALF:P, 2:3]).then_inc(y1_ready, 1)

            def end_layer2(n):
                act.wait_ge(z_used, items_until(n + 1, L2_END))
                wait(act, y2_summed, n)
                relu(y2[:, :], acc2, bias_sb[:, 4:5]).then_inc(y2_ready, 1)

            def high_part(b, it):
                act.wait_ge(z_ready, items_until(b, it))
                wait(act, z_used, items_until(b, it - 2 * RING))
                act.activation(z_hi[:, it // 2 % RING, :, :], z_cut[:, it // 2 % 2, :, :],
                               ACT.Copy).then_inc(hi_ready, 1)

            def step(t, i, b):
                nt, ni = (t, i + 1) if i + 1 < BLOCKS else (t + 1, 0)
                known, par = isinstance(b, int), i % 2
                has = lambda n: not known or 0 <= n < BLOCKS * TILES
                for it in range(1, len(ITEMS), 2):
                    if live(b, it):
                        high_part(b, it)
                    if it == 1 and has(b) and has(b - 1):
                        take_rep(b, par, 3)
                    if it == 3 and has(b - 2):
                        end_layer2(b - 2)
                    if it == 3 and has(b + 1) and ni == 0:
                        take_xs(nt)
                    if it == 5 and has(b + 1):
                        take_x4(b + 1)
                    if it == 11 and has(b + 1):
                        end_layer0(b + 1, 1 - par)
                        take_rep(b + 1, 1 - par, 0)
                    if it == 13 and has(b + 1):
                        take_rep(b + 1, 1 - par, 1)
                    if it == 15 and has(b):
                        end_layer1(b, par)
                    if it == 15 and has(b + 1):
                        take_rep(b + 1, 1 - par, 2)

            act.wait_ge(s_bias, 16)
            take_xs(0)
            take_x4(0)
            end_layer0(0, 0)
            for g in range(GROUPS):
                take_rep(0, 0, g)
            act.wait_ge(w_lo_ready, 1)
            for i in range(BLOCKS):
                step(0, i, i)
            with act.Fori(1, TILES - 1) as t:
                for i in range(BLOCKS):
                    step(t, i, BLOCKS * t + i)
            for b in range(STEPS - 1 - BLOCKS, STEPS):
                step(b // BLOCKS, b % BLOCKS, b)
            end_layer2(STEPS - 2)

            act.wait_ge(s_top, 16 * 8)
            for g in range(4 * MLP_CHUNKS):
                c, m = divmod(g, 4)
                act.wait_ge(m1_acc, g + 1)
                relu(m1[:, m, bass.ts(c, 512)], psum[:, g % 8, :], bt1_sb[:, m:m + 1]).then_inc(m1_ready, 1)
            for g in range(2 * MLP_CHUNKS):
                c, m = divmod(g, 2)
                act.wait_ge(m2_acc, g + 1)
                relu(m2[:, m, bass.ts(c, 512)], psum[:, g, :], bt2_sb[:, m:m + 1]).then_inc(m2_ready, 1)
            for c in range(MLP_CHUNKS):
                act.wait_ge(m3_acc, c + 1)
                act.activation(y_sb[:, bass.ts(c, 512)], psum[0:1, c, :], ACT.Copy).then_inc(m3_ready, 1)

        @block.vector
        def _(dve):
            emb_v = emb[:, :].rearrange("p (r c e) -> p e r c", r=GROUPS, c=FL)

            def cut_parts(t):
                dve.wait_ge(gathered, 16 * FIELDS * (t + 1))
                wait(dve, turned_done, t)
                dve.tensor_copy(parts[:, :, :, 0, :], emb_v).then_inc(cut, 1)
                dve.wait_ge(cut, 4 * t + 1)
                dve.tensor_tensor(rest[:, :, :, :], emb_v, parts[:, :, :, 0, :], ALU.subtract).then_inc(cut, 1)
                dve.wait_ge(cut, 4 * t + 2)
                dve.tensor_copy(parts[:, :, :, 1, :], rest[:, :, :, :]).then_inc(cut, 1)
                dve.wait_ge(cut, 4 * t + 3)
                dve.tensor_tensor(parts[:, :, :, 2, :], rest[:, :, :, :], parts[:, :, :, 1, :],
                                  ALU.subtract).then_inc(cut, 1)

            def shift_products(n, j):
                if j == 0:
                    dve.wait_ge(shift_spread, n + 1)
                    dve.wait_ge(x4_ready, n + 1)
                    wait(dve, l0_done, n)
                dve.tensor_tensor(z0[:, 2 * j:2 * j + 2, :], spread[:, 2 * j:2 * j + 2, :],
                                  x4[:, :].unsqueeze(1).broadcast_to([P, 2, TOK]),
                                  ALU.mult).then_inc(z0_ready, 1)

            def products(b, it, par):
                layer, p = ITEMS[it]
                h, ready, n = (h0[:, par, :], h0_ready, b) if layer == 1 else (h1[:, :], h1_ready, b - 1)
                if p == 0:
                    dve.wait_ge(ready, n + 1)
                if layer == 1 and p % 2 == 0:
                    dve.wait_ge(rep_ready, GROUPS * n + p // 2 + 1)
                if it % 2 == 0:
                    z = z_full[:, it // 2 % RING, :, :]
                    wait(dve, z_used, items_until(b, it - 2 * RING))
                else:
                    z = z_cut[:, it // 2 % 2, :, :]
                    wait(dve, lo_ready, items_until(b, it - 4, odd_only=True))
                m = 2 * (p % 2)
                dve.tensor_tensor(z, xrep[:, par if layer == 1 else 1 - par, p // 2, m:m + 2, :],
                                  h.unsqueeze(1).broadcast_to([P, 2, TOK]),
                                  ALU.mult).then_inc(z_ready, 1)

            def low_part(b, it):
                dve.wait_ge(hi_ready, items_until(b, it, odd_only=True))
                dve.tensor_tensor(z_lo[:, it // 2 % RING, :, :], z_cut[:, it // 2 % 2, :, :],
                                  z_hi[:, it // 2 % RING, :, :].bitcast(F32),
                                  ALU.subtract).then_inc(lo_ready, 1)

            def lane_sum(dst, n, src, done):
                dve.tensor_reduce(dst[:, bass.ts(n, ROWS)], src.rearrange("p (b e) -> p b e", e=EMBED),
                                  AX.X, ALU.add).then_inc(done, 1)

            def step(t, i, b):
                known = isinstance(b, int)
                more = not (known and b + 1 >= BLOCKS * TILES)
                for it in range(len(ITEMS)):
                    if live(b, it):
                        products(b, it, i % 2)
                    if it % 2 == 1:
                        cb, ci = (b, it - 2) if it > 1 else (b - 1, len(ITEMS) - 1)
                        if not (isinstance(cb, int) and cb < 0) and live(cb, ci):
                            low_part(cb, ci)
                    if more and it in DVE_Z0:
                        shift_products(b + 1, DVE_Z0[it])
                    if it == DVE_SUM01 and not (known and b == 0):
                        dve.wait_ge(y0_ready, b)
                        dve.wait_ge(y1_ready, b)
                        lane_sum(cin01, b - 1, y01[:, 1 - i % 2, :], y01_summed)
                    if it == DVE_SUM2 and not (known and b <= 1):
                        dve.wait_ge(y2_ready, b - 1)
                        lane_sum(cin2, b - 2, y2[:, :], y2_summed)
                    if it == DVE_CUT and i == 2 and not (known and b > BLOCKS * (TILES - 1)):
                        cut_parts(t + 1)

            dve.wait_ge(s_sel, 16)
            dve.tensor_copy(sel_sb[:, :, :], sel_f32).then_inc(sel_cast, 1)
            dve.wait_ge(parts_zeroed, 1)
            cut_parts(0)
            dve.wait_ge(s_w0, 32)
            dve.tensor_tensor(w0_sb[:, :, :], w0_sb[:, :, :], w0b_sb, ALU.add).then_inc(w0_summed, 1)
            for j in range(2):
                shift_products(0, j)
            dve.wait_ge(s_w, 32)
            dve.tensor_copy(w_hi[:, :, :, :], w_odd).then_inc(w_hi_ready, 1)
            dve.wait_ge(w_hi_ready, 1)
            dve.tensor_tensor(w_lo[:, :, :, :], w_odd, w_hi[:, :, :, :].bitcast(F32),
                              ALU.subtract).then_inc(w_lo_ready, 1)
            for i in range(BLOCKS):
                step(0, i, i)
            with dve.Fori(1, TILES - 1) as t:
                for i in range(BLOCKS):
                    step(t, i, BLOCKS * t + i)
            for b in range(STEPS - 1 - BLOCKS, STEPS):
                step(b // BLOCKS, b % BLOCKS, b)
            low_part(STEPS - 1, len(ITEMS) - 1)
            dve.wait_ge(y2_ready, STEPS - 1)
            lane_sum(cin2, STEPS - 2, y2[:, :], y2_summed)


def _selections():
    part = np.arange(P) % 32 // FL
    field = FL * (np.arange(P) // 32) + np.arange(P) % FL
    col = np.arange(P)
    live = (part < 3)[:, None]
    mats = [live & ((np.arange(P) % FL)[:, None] == 2 * g + col[None, :] // HALF) for g in range(4)]
    mats.append(live & (field[:, None] == col[None, :] % FIELDS))
    mats += [live & (field[:, None] == (col[None, :] % FIELDS + 4 * j + col[None, :] // FIELDS + 1) % FIELDS)
             for j in range(4)]
    mats.append(col[:, None] == col[None, :])
    return np.ascontiguousarray(np.stack(mats, axis=1).astype(np.float32))


def _shifted_weights(w0):
    w = w0.reshape(CROSS, FIELDS, FIELDS)
    f = np.arange(FIELDS)
    a = np.zeros((KT0, P, CROSS), w0.dtype)
    b = np.zeros((KT0, P, CROSS), w0.dtype)
    for s in range(1, 17):
        j, row = (s - 1) // 4, FIELDS * ((s - 1) % 4)
        a[j, row:row + FIELDS] = w[:, f, (f + s) % FIELDS].T
        if s < 16:
            b[j, row:row + FIELDS] = w[:, (f + s) % FIELDS, f].T
    a[4, 0:FIELDS] = w[:, f, f].T
    return [np.ascontiguousarray(x.transpose(1, 0, 2)) for x in (a, b)]


def kernel(**inputs):
    import concourse.bacc as bacc
    from concourse.bass_utils import run_bass_kernel_spmd

    x = {k: np.asarray(v) for k, v in inputs.items()}
    turn = np.r_[HALF:CROSS, 0:HALF]

    def by_item(first):
        w = {1: x["L0_rec_W1"][turn], 2: x["L0_rec_W2"]}
        w = {n: v.T.reshape(KT, P, CROSS) for n, v in w.items()}
        pairs = [[w[layer][4 * (2 * (p % 2) + m) + p // 2] for m in range(2)]
                 for layer, p in ITEMS[first::2]]
        return np.ascontiguousarray(np.array(pairs).transpose(2, 0, 1, 3))

    w0a, w0b = _shifted_weights(x["L0_rec_W0"])
    b0, b1, b2 = x["L0_rec_b0"], x["L0_rec_b1"], x["L0_rec_b2"]
    bias = np.stack([np.r_[b0[:HALF], b0[:HALF]], np.r_[b0[HALF:], b0[HALF:]],
                     np.r_[b1[:HALF], b1[:HALF]], np.r_[b1[HALF:], b1[HALF:]], b2], axis=1)
    arrays = {
        "ids": x["ids"],
        "dense_t": np.ascontiguousarray(x["dense_ctx"].T),
        "w0a": w0a, "w0b": w0b,
        "w_even": by_item(0), "w_odd_d": by_item(1),
        "bias": np.ascontiguousarray(bias),
        "wt1": x["W_top1"], "wt2": x["W_top2"],
        "wt3": np.ascontiguousarray(x["W_top3"].reshape(TOP2 // P, P).T),
        "bt1": np.ascontiguousarray(x["b_top1"].reshape(TOP1 // P, P).T),
        "bt2": np.ascontiguousarray(x["b_top2"].reshape(TOP2 // P, P).T),
        "sel": _selections(),
    }
    for f in range(FIELDS):
        arrays[f"tbl_{f}"] = x[f"tbl_{f}"]

    nc = bacc.Bacc("TRN2", target_bir_lowering=False, num_devices=1)
    aps = {k: nc.dram_tensor(k, a.shape, mybir.dt.from_np(a.dtype), kind="ExternalInput").ap()
           for k, a in arrays.items()}
    tables = [aps.pop(f"tbl_{f}") for f in range(FIELDS)]
    out = nc.dram_tensor("out", (1, BATCH), F32, kind="ExternalOutput").ap()
    build(nc, tables=tables, out=out, **aps)
    r = run_bass_kernel_spmd(nc, [arrays], core_ids=[0])
    return np.asarray(r.results[0]["out"]).reshape(BATCH, 1)
```

```python
from contextlib import ExitStack

import numpy as np

import concourse.bass as bass
import concourse.mybir as mybir
from concourse.alu_op_type import AluOpType as ALU

ACT = mybir.ActivationFunctionType
AX = mybir.AxisListType
F32 = mybir.dt.float32
F32R = mybir.dt.float32r
BF16 = mybir.dt.bfloat16
I32 = mybir.dt.int32

P = 128
BATCH = 2048
FIELDS = 32
EMBED = 16
CROSS = 128
HALF = CROSS // 2
DENSE = 16
TOP1, TOP2 = 512, 256

TILES = BATCH // P
BLOCKS = 4
ROWS = P // BLOCKS
TOK = ROWS * EMBED

KT = FIELDS * HALF // P
GROUPS = 4
SOURCES = 2
SOURCE_TILES = KT // SOURCES
PAIRS = KT // 2
KT0 = 5
STEPS = TILES * BLOCKS + 1

ITEMS = ([(1, 0), (1, 1), (1, 2)] + [x for p in range(5) for x in ((2, p), (1, p + 3))]
         + [(2, 5), (2, 6), (2, 7)])
L1_END, L2_END = ITEMS.index((1, PAIRS - 1)), ITEMS.index((2, PAIRS - 1))
ALL = tuple(range(len(ITEMS)))
CUT = (1, 3, 5, 9, 11, 13, 15)
FULL = tuple(it for it in ALL if it not in CUT)
RING = 4
CUT_RING = 2

PE_TURN = 1
PE_X4, PE_LAYER0 = (1, 3), (9, 11)
PE_SOURCE = 5
LOW_AFTER = 2
DVE_Z0 = (9, 10)
DVE_SUM01, DVE_SUM2, DVE_CUT = 5, 6, 13
TOP1_AT = (8, 10, 12, 14)
ACT_X4, ACT_LAYER0 = (3, 5), (11, 13)
ACT_SOURCE = 7
ACT_LAYER1, ACT_LAYER2 = 15, 3

SELS = 3 + SOURCES
PARTS = 4
FL = FIELDS // GROUPS
MLP_CHUNKS = BATCH // 512


def build(nc, ids, tables, dense_t, w0a, w0b, w_whole, w_cut, bias, wt1, wt2, wt3, bt1, bt2, sel, out):
    with ExitStack() as ctx:
        def sb(name, shape, dt=F32):
            return ctx.enter_context(nc.sbuf_tensor(name, shape, dt))

        def sem(name):
            return ctx.enter_context(nc.semaphore(name))

        w0_sb = sb("w0_sb", [P, KT0, CROSS])
        w_full = sb("w_full", [P, len(FULL), 2, CROSS])
        w_hi = sb("w_hi", [P, len(CUT), 2, CROSS], F32R)
        w_lo = sb("w_lo", [P, len(CUT), 2, CROSS], F32R)
        bias_sb = sb("bias_sb", [P, 5])
        wt3_sb = sb("wt3_sb", [P, TOP2 // P])
        bt1_sb = sb("bt1_sb", [P, TOP1 // P])
        bt2_sb = sb("bt2_sb", [P, TOP2 // P])
        sel_sb = sb("sel_sb", [P, SELS, P], BF16)
        sel_x4 = sel_sb[:, 0, :]
        sel_next = sel_sb[:, 1, :]
        sel_source = sel_sb[:, 2:2 + SOURCES, :]
        ident = sel_sb[:, 2 + SOURCES, :]

        ids_sb = sb("ids_sb", [P, FIELDS], I32)
        emb = sb("emb", [P, FIELDS * EMBED])
        rest = sb("rest", [P, EMBED, GROUPS, FL])
        parts = sb("parts", [P, EMBED, GROUPS, PARTS, FL], BF16)
        xs = sb("xs", [P, P, EMBED], BF16)

        x4 = sb("x4", [P, TOK])
        source = sb("source", [P, SOURCES, TOK])
        xrep = sb("xrep", [P, 2, GROUPS, GROUPS, TOK])
        z0 = sb("z0", [P, 4, TOK])
        zsq = sb("zsq", [P, TOK])
        z_full = sb("z_full", [P, RING, 2, TOK])
        z_cut = sb("z_cut", [P, CUT_RING, 2, TOK])
        z_hi = sb("z_hi", [P, RING, 2, TOK], F32R)
        z_lo = sb("z_lo", [P, RING, 2, TOK], F32R)
        h0 = sb("h0", [P, 2, TOK])
        h1 = sb("h1", [P, TOK])
        y01 = sb("y01", [P, 2, TOK])
        y2 = sb("y2", [P, TOK])

        cin01 = sb("cin01", [P, BATCH])
        cin2 = sb("cin2", [P, BATCH])

        even = xrep[:, 0, :, :, :].rearrange("p b c t -> p (b c t)")
        odd = xrep[:, 1, :, :, :].rearrange("p b c t -> p (b c t)")
        sel_f32 = odd[:, 0:SELS * P].rearrange("p (m c) -> p m c", m=SELS)
        w0b_sb = odd[:, SELS * P:(SELS + KT0) * P].rearrange("p (k c) -> p k c", k=KT0)
        w_staged = odd[:, 2048:2048 + len(CUT) * 2 * CROSS].rearrange("p (i m c) -> p i m c", m=2, c=CROSS)
        wt1_sb = even[:, 0:3 * TOP1].rearrange("p (k n) -> p k n", k=3)
        wt2_sb = even[:, 2048:2048 + 4 * TOP2].rearrange("p (k n) -> p k n", k=4)
        dense_sb = even[0:DENSE, 4096:4096 + BATCH]
        y_sb = even[0:1, 6144:6144 + BATCH]
        m1_rest = odd.rearrange("p (c m b) -> p c m b", c=4, m=4)
        m1 = [z0[:, :, :]] + [m1_rest[:, c, :, :] for c in range(1, MLP_CHUNKS)]
        m2 = z_full[:, :, :, :].rearrange("p a m t -> p (a m t)").rearrange("p (m b) -> p m b", m=2)

        psum = ctx.enter_context(nc.psum_tensor("psum", [P, 8, 512], F32))
        spread = psum[:, 0:SOURCES, :]
        acc0, acc1, acc2 = psum[:, 4, :], psum[:, 5, :], psum[:, 6, :]
        misc = psum[:, 7, :]
        turned = [x.bitcast(BF16).rearrange("p (e b) -> p e b", e=8) for x in (misc, psum[:, 0, :])]

        s_sel, s_w0, s_bias = sem("s_sel"), sem("s_w0"), sem("s_bias")
        s_w, s_top = sem("s_w"), sem("s_top")
        ids_loaded = sem("ids_loaded")
        tiles_begun = sem("tiles_begun")
        gathered = sem("gathered")
        parts_zeroed = sem("parts_zeroed")
        cut = sem("cut")
        turned_done = sem("turned_done")
        xs_ready = sem("xs_ready")
        sel_cast = sem("sel_cast")
        w0_summed = sem("w0_summed")
        w_hi_ready = sem("w_hi_ready")
        w_lo_ready = sem("w_lo_ready")
        x4_spread = sem("x4_spread")
        x4_ready = sem("x4_ready")
        zsq_ready = sem("zsq_ready")
        next_spread = sem("next_spread")
        next_ready = sem("next_ready")
        shifted = sem("shifted")
        z0_ready = sem("z0_ready")
        source_spread = sem("source_spread")
        source_ready = sem("source_ready")
        rep_copied = [sem(f"rep_copied_{g}") for g in range(GROUPS)]
        z_ready = sem("z_ready")
        hi_ready = sem("hi_ready")
        lo_ready = sem("lo_ready")
        z_used = sem("z_used")
        l0_done = sem("l0_done")
        h0_ready, h1_ready = sem("h0_ready"), sem("h1_ready")
        y0_ready = sem("y0_ready")
        y1_ready = sem("y1_ready")
        y2_ready = sem("y2_ready")
        y01_summed, y2_summed = sem("y01_summed"), sem("y2_summed")
        m1_acc, m1_ready = sem("m1_acc"), sem("m1_ready")
        m2_acc, m2_ready = sem("m2_acc"), sem("m2_ready")
        m3_acc, m3_ready = sem("m3_acc"), sem("m3_ready")
        stored = sem("stored")

        def wait(eng, semaphore, value):
            if not isinstance(value, int) or value > 0:
                eng.wait_ge(semaphore, value)

        def live(b, it):
            return not (isinstance(b, int) and (b == 0 and ITEMS[it][0] == 2
                                                or b == STEPS - 1 and ITEMS[it][0] == 1))

        def items_until(b, it, kind=ALL):
            if isinstance(b, int) and b < 0:
                return 0
            here = sum(live(b, j) for j in kind if j <= it)
            if isinstance(b, int) and b == 0:
                return here
            return len(kind) * (b - 1) + sum(live(0, j) for j in kind) + here

        def back(b, it, n, kind):
            steps, at = divmod(kind.index(it) - n, len(kind))
            return b + steps, kind[at]

        def slot(i, it, kind, ring):
            return (len(kind) * i + kind.index(it)) % ring

        block = ctx.enter_context(nc.Block())

        @block.sync
        def _(sp):
            ids_v = ids.rearrange("(t p) f -> t p f", p=P)
            sp.dma_start(ids_sb[:, :], ids_v[0]).then_inc(ids_loaded, 16)
            sp.dma_start(sel_f32, sel).then_inc(s_sel, 16)
            sp.dma_start(w0_sb[:, :, :], w0a).then_inc(s_w0, 16)
            sp.dma_start(w0b_sb, w0b).then_inc(s_w0, 16)
            sp.dma_start(bias_sb[:, :], bias).then_inc(s_bias, 16)
            sp.dma_start(w_full[:, :, :, :], w_whole).then_inc(s_w, 16)
            sp.dma_start(w_staged, w_cut).then_inc(s_w, 16)
            sp.dma_start(wt3_sb[:, :], wt3).then_inc(s_top, 16)
            sp.dma_start(bt1_sb[:, :], bt1).then_inc(s_top, 16)
            sp.dma_start(bt2_sb[:, :], bt2).then_inc(s_top, 16)

            def load_ids(t):
                sp.wait_ge(gathered, t * (16 * FIELDS))
                sp.wait_ge(cut, 4 * t - 2)
                sp.dma_start(ids_sb[:, :], ids[bass.ts(t, P), :]).then_inc(ids_loaded, 16)

            def shift_x(n):
                sp.wait_ge(next_ready, n + 1)
                wait(sp, l0_done, n)
                for j in range(1, 4):
                    d = 4 * 4 * j
                    sp.dma_start(z0[0:P - d, j, :], z0[d:P, 0, :]).then_inc(shifted, 16)
                    sp.dma_start(z0[P - d:P, j, :], z0[0:d, 0, :]).then_inc(shifted, 16)

            def copy_rep(n, par):
                sp.wait_ge(source_ready, n + 1)
                for g in range(GROUPS):
                    wait(sp, z_ready, items_until(n - 1, ITEMS.index((2, 2 * g + 1))))
                    for r in (0, 2, 1, 3):
                        sp.dma_start(xrep[:, par, g, r, :],
                                     source[2 * r + g % 2::SOURCE_TILES, g // 2, :].unsqueeze(1)
                                     .broadcast_to([P // SOURCE_TILES, SOURCE_TILES, TOK])
                                     ).then_inc(rep_copied[g], 16)

            def prepare(n, par):
                shift_x(n)
                copy_rep(n, par)

            prepare(0, 0)
            load_ids(1)
            sp.wait_ge(w_lo_ready, 1)
            sp.wait_ge(sel_cast, 1)
            for i in range(1, BLOCKS):
                prepare(i, i % 2)
            with sp.Fori(1, TILES - 1) as t:
                prepare(BLOCKS * t, 0)
                load_ids(t + 1)
                for i in range(1, BLOCKS):
                    prepare(BLOCKS * t + i, i % 2)
            for n in range(BLOCKS * (TILES - 1), BLOCKS * TILES):
                prepare(n, n % 2)
            sp.wait_ge(z_ready, items_until(STEPS - 2, L2_END))
            for k in range(2):
                sp.dma_start(wt1_sb[:, k, :], wt1[k * P:(k + 1) * P, :]).then_inc(s_top, 16)
            sp.dma_start(wt1_sb[0:DENSE, 2, :], wt1[2 * P:2 * P + DENSE, :]).then_inc(s_top, 16)
            sp.dma_start(wt2_sb, wt2.rearrange("(k p) n -> p k n", p=P)).then_inc(s_top, 16)
            sp.dma_start(dense_sb, dense_t).then_inc(s_top, 16)
            for c in range(MLP_CHUNKS):
                sp.wait_ge(m3_ready, c + 1)
                sp.dma_start(out[0:1, bass.ts(c, 512)], y_sb[:, bass.ts(c, 512)]).then_inc(stored, 16)
            sp.wait_ge(stored, 16 * MLP_CHUNKS)

        @block.gpsimd
        def _(pool):
            pool.memset(parts[:, :, :, 3, :], 0.0).then_inc(parts_zeroed, 1)

            def gather_fields():
                for f in range(FIELDS):
                    pool.indirect_dma_start(
                        out=emb[:, f * EMBED:(f + 1) * EMBED], out_offset=None,
                        in_=tables[f], in_offset=bass.IndirectOffsetOnAxis(ids_sb[:, f:f + 1], 0),
                    ).then_inc(gathered, 16)

            pool.wait_ge(ids_loaded, 16)
            gather_fields()
            with pool.Fori(1, TILES) as t:
                pool.wait_ge(ids_loaded, 16 * t + 16)
                pool.sem_inc(tiles_begun, 1)
                gather_fields()

        @block.tensor
        def _(pe):
            def turn(t):
                pe.wait_ge(cut, 4 * t + 4)
                wait(pe, zsq_ready, BLOCKS * t)
                wait(pe, source_ready, BLOCKS * t)
                for e in range(EMBED):
                    lane = parts[:, e].rearrange("p a b c -> p (a b c)")
                    mm = pe.transpose(turned[e // 8][:, e % 8, :], lane, ident)
                mm.then_inc(turned_done, 1)

            def tokens(i, lo, hi):
                return xs[lo:hi, ROWS * i:ROWS * (i + 1), :].rearrange("p b e -> p (b e)")

            def spread_x4(t, i, n):
                pe.wait_ge(xs_ready, 2 * t + 2)
                wait(pe, y0_ready, n)
                pe.matmul(acc0, sel_next, tokens(i, 0, P), start=True, stop=True).then_inc(next_spread, 1)
                wait(pe, zsq_ready, n)
                pe.matmul(misc, sel_x4, tokens(i, 0, P), start=True, stop=True).then_inc(x4_spread, 1)

            def spread_source(i, n):
                wait(pe, source_ready, n)
                for k in range(SOURCES):
                    mm = pe.matmul(spread[:, k, :], sel_source[:, k, :], tokens(i, 0, P),
                                   start=True, stop=True)
                mm.then_inc(source_spread, 1)

            def layer0(n):
                pe.wait_ge(zsq_ready, n + 1)
                pe.wait_ge(next_ready, n + 1)
                pe.matmul(acc0, w0_sb[:, 4, :], zsq[:, :], start=True, stop=False)
                for j in range(4):
                    if j % 2 == 0:
                        pe.wait_ge(z0_ready, 2 * n + j // 2 + 1)
                    mm = pe.matmul(acc0, w0_sb[:, j, :], z0[:, j, :], start=False, stop=(j == 3))
                mm.then_inc(l0_done, 1)

            def contract(i, b, it):
                layer, p = ITEMS[it]
                acc = acc1 if layer == 1 else acc2
                if p == 0 and layer == 1:
                    wait(pe, y1_ready, b)
                if p == 0 and layer == 2:
                    wait(pe, y2_ready, b - 1)
                first, last = p == 0, p == PAIRS - 1
                if it in FULL:
                    w, z = FULL.index(it), slot(i, it, FULL, RING)
                    pe.wait_ge(z_ready, items_until(b, it))
                    for m in range(2):
                        mm = pe.matmul(acc, w_full[:, w, m, :], z_full[:, z, m, :],
                                       start=(first and m == 0), stop=(last and m == 1))
                else:
                    w, z = CUT.index(it), slot(i, it, CUT, RING)
                    pe.wait_ge(hi_ready, items_until(b, it, CUT))
                    for m in range(2):
                        pe.matmul(acc, w_hi[:, w, m, :], z_hi[:, z, m, :],
                                  start=(first and m == 0), stop=False)
                        pe.matmul(acc, w_lo[:, w, m, :], z_hi[:, z, m, :],
                                  start=False, stop=False)
                    pe.wait_ge(lo_ready, items_until(b, it, CUT))
                    for m in range(2):
                        mm = pe.matmul(acc, w_hi[:, w, m, :], z_lo[:, z, m, :],
                                       start=False, stop=(last and m == 1))
                mm.then_inc(z_used, 1)

            def top1(c, m):
                g, rows, cols = 4 * c + m, bass.ts(c, 512), bass.ts(m, P)
                pe.wait_ge(s_top, 16 * 8)
                pe.wait_ge(y01_summed, 512 // ROWS * (c + 1))
                pe.wait_ge(y2_summed, 512 // ROWS * (c + 1))
                if g < 4:
                    pe.wait_ge(source_ready, BLOCKS * TILES)
                else:
                    pe.wait_ge(y2_ready, BLOCKS * TILES)
                wait(pe, m1_ready, g - 7)
                pe.matmul(psum[:, g % 8, :], wt1_sb[:, 0, cols], cin01[:, rows], start=True, stop=False)
                pe.matmul(psum[:, g % 8, :], wt1_sb[:, 1, cols], cin2[:, rows], start=False, stop=False)
                pe.matmul(psum[:, g % 8, :], wt1_sb[0:DENSE, 2, cols], dense_sb[:, rows],
                          start=False, stop=True).then_inc(m1_acc, 1)

            def step(t, i, b):
                nt, ni = (t, i + 1) if i + 1 < BLOCKS else (t + 1, 0)
                more = not (isinstance(b, int) and b + 1 >= BLOCKS * TILES)
                for it in range(len(ITEMS)):
                    if more and it == PE_TURN and ni == 0:
                        turn(nt)
                    if more and it == PE_X4[ni == 0]:
                        spread_x4(nt, ni, b + 1)
                    if more and it == PE_SOURCE:
                        spread_source(ni, b + 1)
                    if more and it == PE_LAYER0[ni == 0]:
                        layer0(b + 1)
                    if not more and b == STEPS - 1 and it in TOP1_AT:
                        top1(0, TOP1_AT.index(it))
                    if live(b, it):
                        contract(i, b, it)

            pe.wait_ge(sel_cast, 1)
            turn(0)
            spread_x4(0, 0, 0)
            spread_source(0, 0)
            pe.wait_ge(w0_summed, 1)
            layer0(0)
            pe.wait_ge(s_w, 32)
            pe.wait_ge(w_lo_ready, 1)
            for i in range(BLOCKS):
                step(0, i, i)
            with pe.Fori(1, TILES - 1) as t:
                for i in range(BLOCKS):
                    step(t, i, BLOCKS * t + i)
            for b in range(STEPS - 1 - BLOCKS, STEPS):
                step(b // BLOCKS, b % BLOCKS, b)

            for c in range(1, MLP_CHUNKS):
                for m in range(TOP1 // P):
                    top1(c, m)
            for c in range(MLP_CHUNKS):
                rows = bass.ts(c, 512)
                pe.wait_ge(m1_ready, 4 * (c + 1))
                for m in range(TOP2 // P):
                    g = 2 * c + m
                    pe.wait_ge(m1_ready, 8 + g + 1)
                    for k in range(4):
                        mm = pe.matmul(psum[:, g, :], wt2_sb[:, k, bass.ts(m, P)], m1[c][:, k, :],
                                       start=(k == 0), stop=(k == 3))
                    mm.then_inc(m2_acc, 1)
            for c in range(MLP_CHUNKS):
                pe.wait_ge(m2_ready, 2 * (c + 1))
                for k in range(2):
                    mm = pe.matmul(psum[0:1, c, :], wt3_sb[:, k:k + 1], m2[:, k, bass.ts(c, 512)],
                                   start=(k == 0), stop=(k == 1))
                mm.then_inc(m3_acc, 1)

        @block.scalar
        def _(act):
            def take_xs(t):
                act.wait_ge(turned_done, t + 1)
                for half in range(2):
                    act.activation(xs[:, :, 8 * half:8 * half + 8].rearrange("p b e -> p e b"),
                                   turned[half], ACT.Copy).then_inc(xs_ready, 1)

            def take_x4(n):
                act.wait_ge(next_spread, n + 1)
                wait(act, l0_done, n)
                act.activation(z0[:, 0, :], acc0, ACT.Copy).then_inc(next_ready, 1)
                act.wait_ge(x4_spread, n + 1)
                wait(act, z0_ready, 2 * n)
                act.activation(x4[:, :], misc, ACT.Copy).then_inc(x4_ready, 1)
                act.activation(zsq[:, :], misc, ACT.Square).then_inc(zsq_ready, 1)

            def take_source(n):
                act.wait_ge(source_spread, n + 1)
                for copied in rep_copied:
                    wait(act, copied, 4 * 16 * n)
                act.activation(source[:, :, :], spread, ACT.Copy).then_inc(source_ready, 1)

            def relu(out_, in_, b):
                return act.activation(out_, in_, ACT.Relu, bias=b)

            def end_layer0(n, par):
                act.wait_ge(l0_done, n + 1)
                wait(act, z_ready, items_until(n - 2, L1_END))
                relu(h0[HALF:P, par, :], acc0[HALF:P, :], bias_sb[HALF:P, 1:2])
                relu(h0[0:HALF, par, :], acc0[HALF:P, :], bias_sb[HALF:P, 1:2]).then_inc(h0_ready, 1)
                wait(act, y01_summed, n - 1)
                relu(y01[0:HALF, par, :], acc0[0:HALF, :], bias_sb[0:HALF, 0:1]).then_inc(y0_ready, 1)

            def end_layer1(n, par):
                act.wait_ge(z_used, items_until(n, L1_END))
                wait(act, z_ready, items_until(n, L2_END))
                relu(h1[0:HALF, :], acc1[0:HALF, :], bias_sb[0:HALF, 3:4])
                relu(h1[HALF:P, :], acc1[0:HALF, :], bias_sb[0:HALF, 3:4]).then_inc(h1_ready, 1)
                relu(y01[HALF:P, par, :], acc1[HALF:P, :], bias_sb[HALF:P, 2:3]).then_inc(y1_ready, 1)

            def end_layer2(n):
                act.wait_ge(z_used, items_until(n + 1, L2_END))
                wait(act, y2_summed, n)
                relu(y2[:, :], acc2, bias_sb[:, 4:5]).then_inc(y2_ready, 1)

            def high_part(i, b, it):
                act.wait_ge(z_ready, items_until(b, it))
                wait(act, z_used, items_until(*back(b, it, RING, CUT)))
                act.activation(z_hi[:, slot(i, it, CUT, RING), :, :],
                               z_cut[:, slot(i, it, CUT, CUT_RING), :, :],
                               ACT.Copy).then_inc(hi_ready, 1)

            def end_top1(c, m):
                act.wait_ge(s_top, 16 * 8)
                act.wait_ge(m1_acc, 4 * c + m + 1)
                relu(m1[c][:, m, :], psum[:, (4 * c + m) % 8, :], bt1_sb[:, m:m + 1]).then_inc(m1_ready, 1)

            def step(t, i, b):
                nt, ni = (t, i + 1) if i + 1 < BLOCKS else (t + 1, 0)
                known, par = isinstance(b, int), i % 2
                has = lambda n: not known or 0 <= n < BLOCKS * TILES
                for it in ALL:
                    if it in CUT and live(b, it):
                        high_part(i, b, it)
                    if it == 3 and has(b + 1) and ni == 0:
                        take_xs(nt)
                    if it == ACT_X4[ni == 0] and has(b + 1):
                        take_x4(b + 1)
                    if it == ACT_SOURCE and has(b + 1):
                        take_source(b + 1)
                    if known and b == STEPS - 1 and it - 1 in TOP1_AT:
                        end_top1(0, TOP1_AT.index(it - 1))
                    if it == ACT_LAYER2 and has(b - 2):
                        end_layer2(b - 2)
                    if it == ACT_LAYER1 and has(b):
                        end_layer1(b, par)
                    if it == ACT_LAYER0[ni == 0] and has(b + 1):
                        end_layer0(b + 1, 1 - par)

            act.wait_ge(s_sel, 16)
            act.activation(sel_sb[:, :, :], sel_f32, ACT.Copy).then_inc(sel_cast, 1)
            act.wait_ge(s_bias, 16)
            take_xs(0)
            take_x4(0)
            take_source(0)
            end_layer0(0, 0)
            for i in range(BLOCKS):
                step(0, i, i)
            with act.Fori(1, TILES - 1) as t:
                for i in range(BLOCKS):
                    step(t, i, BLOCKS * t + i)
            for b in range(STEPS - 1 - BLOCKS, STEPS):
                step(b // BLOCKS, b % BLOCKS, b)
            end_layer2(STEPS - 2)

            for c in range(1, MLP_CHUNKS):
                for m in range(TOP1 // P):
                    end_top1(c, m)
            for g in range(2 * MLP_CHUNKS):
                c, m = divmod(g, 2)
                act.wait_ge(m2_acc, g + 1)
                relu(m2[:, m, bass.ts(c, 512)], psum[:, g, :], bt2_sb[:, m:m + 1]).then_inc(m2_ready, 1)
            for c in range(MLP_CHUNKS):
                act.wait_ge(m3_acc, c + 1)
                act.activation(y_sb[:, bass.ts(c, 512)], psum[0:1, c, :], ACT.Copy).then_inc(m3_ready, 1)

        @block.vector
        def _(dve):
            emb_v = emb[:, :].rearrange("p (r c e) -> p e r c", r=GROUPS, c=FL)

            def cut_parts(t):
                dve.wait_ge(gathered, 16 * FIELDS * (t + 1))
                wait(dve, turned_done, t)
                dve.tensor_copy(parts[:, :, :, 0, :], emb_v).then_inc(cut, 1)
                dve.wait_ge(cut, 4 * t + 1)
                dve.tensor_tensor(rest[:, :, :, :], emb_v, parts[:, :, :, 0, :], ALU.subtract).then_inc(cut, 1)
                dve.wait_ge(cut, 4 * t + 2)
                dve.tensor_copy(parts[:, :, :, 1, :], rest[:, :, :, :]).then_inc(cut, 1)
                dve.wait_ge(cut, 4 * t + 3)
                dve.tensor_tensor(parts[:, :, :, 2, :], rest[:, :, :, :], parts[:, :, :, 1, :],
                                  ALU.subtract).then_inc(cut, 1)

            def shift_products(n, j):
                if j == 0:
                    dve.wait_ge(x4_ready, n + 1)
                    dve.wait_ge(shifted, 6 * 16 * (n + 1))
                dve.tensor_tensor(z0[:, 2 * j:2 * j + 2, :], z0[:, 2 * j:2 * j + 2, :],
                                  x4[:, :].unsqueeze(1).broadcast_to([P, 2, TOK]),
                                  ALU.mult).then_inc(z0_ready, 1)

            def products(i, b, it):
                layer, p = ITEMS[it]
                par = i % 2
                h, ready, n = (h0[:, par, :], h0_ready, b) if layer == 1 else (h1[:, :], h1_ready, b - 1)
                if p == 0:
                    dve.wait_ge(ready, n + 1)
                if layer == 1 and p % 2 == 0:
                    dve.wait_ge(rep_copied[p // 2], 4 * 16 * (n + 1))
                if it in FULL:
                    z = z_full[:, slot(i, it, FULL, RING), :, :]
                    wait(dve, z_used, items_until(*back(b, it, RING, FULL)))
                else:
                    z = z_cut[:, slot(i, it, CUT, CUT_RING), :, :]
                    before = back(b, it, CUT_RING, CUT)
                    wait(dve, lo_ready, items_until(*before, CUT))
                m = 2 * (p % 2)
                dve.tensor_tensor(z, xrep[:, par if layer == 1 else 1 - par, p // 2, m:m + 2, :],
                                  h.unsqueeze(1).broadcast_to([P, 2, TOK]),
                                  ALU.mult).then_inc(z_ready, 1)

            def low_part(i, b, it):
                dve.wait_ge(hi_ready, items_until(b, it, CUT))
                z = slot(i, it, CUT, RING)
                dve.tensor_tensor(z_lo[:, z, :, :], z_cut[:, slot(i, it, CUT, CUT_RING), :, :],
                                  z_hi[:, z, :, :].bitcast(F32),
                                  ALU.subtract).then_inc(lo_ready, 1)

            def lane_sum(dst, n, src, done):
                dve.tensor_reduce(dst[:, bass.ts(n, ROWS)], src.rearrange("p (b e) -> p b e", e=EMBED),
                                  AX.X, ALU.add).then_inc(done, 1)

            def step(t, i, b):
                known = isinstance(b, int)
                more = not (known and b + 1 >= BLOCKS * TILES)
                for it in range(len(ITEMS)):
                    if live(b, it):
                        products(i, b, it)
                    over, made = divmod(it - LOW_AFTER, len(ITEMS))
                    if made in CUT and not (known and b + over < 0) and live(b + over, made):
                        low_part(i + over, b + over, made)
                    z0_at = DVE_Z0[i == BLOCKS - 1]
                    if more and it in (z0_at, z0_at + 1):
                        shift_products(b + 1, it - z0_at)
                    if it == DVE_SUM01 and not (known and b == 0):
                        dve.wait_ge(y0_ready, b)
                        dve.wait_ge(y1_ready, b)
                        lane_sum(cin01, b - 1, y01[:, 1 - i % 2, :], y01_summed)
                    if it == DVE_SUM2 and not (known and b <= 1):
                        dve.wait_ge(y2_ready, b - 1)
                        lane_sum(cin2, b - 2, y2[:, :], y2_summed)
                    if it == DVE_CUT and i == 2 and not (known and b > BLOCKS * (TILES - 1)):
                        cut_parts(t + 1)

            dve.wait_ge(s_w0, 32)
            dve.tensor_tensor(w0_sb[:, :, :], w0_sb[:, :, :], w0b_sb, ALU.add).then_inc(w0_summed, 1)
            dve.wait_ge(s_w, 32)
            dve.tensor_copy(w_hi[:, :, :, :], w_staged).then_inc(w_hi_ready, 1)
            dve.wait_ge(w_hi_ready, 1)
            dve.tensor_tensor(w_lo[:, :, :, :], w_staged, w_hi[:, :, :, :].bitcast(F32),
                              ALU.subtract).then_inc(w_lo_ready, 1)
            dve.wait_ge(parts_zeroed, 1)
            cut_parts(0)
            for j in range(2):
                shift_products(0, j)
            for i in range(BLOCKS):
                step(0, i, i)
            with dve.Fori(1, TILES - 1) as t:
                for i in range(BLOCKS):
                    step(t, i, BLOCKS * t + i)
            for b in range(STEPS - 1 - BLOCKS, STEPS):
                step(b // BLOCKS, b % BLOCKS, b)
            for it in CUT:
                if it + LOW_AFTER >= len(ITEMS):
                    low_part(STEPS - 1, STEPS - 1, it)
            dve.wait_ge(y2_ready, STEPS - 1)
            lane_sum(cin2, STEPS - 2, y2[:, :], y2_summed)


def _selections():
    part = np.arange(P) % 32 // FL
    field = FL * (np.arange(P) // 32) + np.arange(P) % FL
    col = np.arange(P)
    live = (part < 3)[:, None]
    mats = [live & (field[:, None] == col[None, :] // 4)]
    mats.append(live & (field[:, None] == (col[None, :] // 4 + col[None, :] % 4 + 1) % FIELDS))
    k, second = col % SOURCE_TILES, col // HALF
    for source in range(SOURCES):
        first = FL * (k // 2) + 2 * (2 * source + k % 2)
        mats.append(live & (field[:, None] == (first + second)[None, :]))
    mats.append(col[:, None] == col[None, :])
    return np.ascontiguousarray(np.stack(mats, axis=1).astype(np.float32))


def _shifted_weights(w0):
    w = w0.reshape(CROSS, FIELDS, FIELDS)
    f = np.arange(FIELDS)
    a = np.zeros((KT0, P, CROSS), w0.dtype)
    b = np.zeros((KT0, P, CROSS), w0.dtype)
    for s in range(1, 17):
        j, sub = divmod(s - 1, 4)
        a[j, sub::4] = w[:, f, (f + s) % FIELDS].T
        if s < 16:
            b[j, sub::4] = w[:, (f + s) % FIELDS, f].T
    a[4, 0::4] = w[:, f, f].T
    return [np.ascontiguousarray(x.transpose(1, 0, 2)) for x in (a, b)]


def kernel(**inputs):
    import concourse.bacc as bacc
    from concourse.bass_utils import run_bass_kernel_spmd

    x = {k: np.asarray(v) for k, v in inputs.items()}
    turn = np.r_[HALF:CROSS, 0:HALF]

    def by_item(kind):
        w = {1: x["L0_rec_W1"][turn], 2: x["L0_rec_W2"]}
        w = {n: v.T.reshape(KT, P, CROSS) for n, v in w.items()}
        pairs = [[w[layer][4 * (2 * (p % 2) + m) + p // 2] for m in range(2)]
                 for layer, p in (ITEMS[it] for it in kind)]
        return np.ascontiguousarray(np.array(pairs).transpose(2, 0, 1, 3))

    w0a, w0b = _shifted_weights(x["L0_rec_W0"])
    b0, b1, b2 = x["L0_rec_b0"], x["L0_rec_b1"], x["L0_rec_b2"]
    bias = np.stack([np.r_[b0[:HALF], b0[:HALF]], np.r_[b0[HALF:], b0[HALF:]],
                     np.r_[b1[:HALF], b1[:HALF]], np.r_[b1[HALF:], b1[HALF:]], b2], axis=1)
    arrays = {
        "ids": x["ids"],
        "dense_t": np.ascontiguousarray(x["dense_ctx"].T),
        "w0a": w0a, "w0b": w0b,
        "w_whole": by_item(FULL), "w_cut": by_item(CUT),
        "bias": np.ascontiguousarray(bias),
        "wt1": x["W_top1"], "wt2": x["W_top2"],
        "wt3": np.ascontiguousarray(x["W_top3"].reshape(TOP2 // P, P).T),
        "bt1": np.ascontiguousarray(x["b_top1"].reshape(TOP1 // P, P).T),
        "bt2": np.ascontiguousarray(x["b_top2"].reshape(TOP2 // P, P).T),
        "sel": _selections(),
    }
    for f in range(FIELDS):
        arrays[f"tbl_{f}"] = x[f"tbl_{f}"]

    nc = bacc.Bacc("TRN2", target_bir_lowering=False, num_devices=1)
    aps = {k: nc.dram_tensor(k, a.shape, mybir.dt.from_np(a.dtype), kind="ExternalInput").ap()
           for k, a in arrays.items()}
    tables = [aps.pop(f"tbl_{f}") for f in range(FIELDS)]
    out = nc.dram_tensor("out", (1, BATCH), F32, kind="ExternalOutput").ap()
    build(nc, tables=tables, out=out, **aps)
    r = run_bass_kernel_spmd(nc, [arrays], core_ids=[0])
    return np.asarray(r.results[0]["out"]).reshape(BATCH, 1)
```
